# Optimizing a Trainium2 kernel written in Bass

```python
import numpy as np
import jax
import jax.numpy as jnp

def _softmax(x, axis=-1):
    return jax.nn.softmax(x, axis=axis)

def _gelu(x):
    return jax.nn.gelu(x, approximate=True)

def _silu(x):
    return jax.nn.silu(x)

def _sigmoid(x):
    return jax.nn.sigmoid(x)

def _layernorm(x, axis=-1, eps=1e-05):
    m = jnp.mean(x, axis=axis, keepdims=True)
    v = jnp.var(x, axis=axis, keepdims=True)
    return (x - m) / jnp.sqrt(v + eps)

def _scatter_add(tgt, idx, src, axis=0):
    return tgt.at[idx].add(src)

def _segment_sum(src, seg, n):
    return jax.ops.segment_sum(src, seg, n)
kernel_name = 'mk_lm_tower_d1_tok_ids2048_r4_2ecb7e'

def setup_inputs(seed: int=0):
    np.random.seed(seed)
    _w = jnp.asarray

    def _rec_inputs():
        import jax
        import jax.numpy as jnp
        _rk = jax.random.key(seed)
        x = jax.random.randint(jax.random.fold_in(_rk, 1), (16, 128), 0, 127990, jnp.int32)
        return x
    x = _rec_inputs()

    def _L0_tok_setup():
        import jax, jax.numpy as jnp
        import numpy as np
        VOCAB = 32000
        EMBED = 512
        N_TRAIN = 64
        BATCH, SEQ = (4, 1024)
        key = jax.random.key(seed)
        k1, k2, k3, k4 = jax.random.split(key, 4)
        x = jax.random.randint(k1, (BATCH, SEQ), 0, VOCAB, dtype=jnp.int64 if jax.config.jax_enable_x64 else jnp.int32)
        W = jax.random.normal(k2, (VOCAB, EMBED), dtype=jnp.float32)
        delta_values = jax.random.normal(k3, (N_TRAIN * EMBED,), dtype=jnp.float32)
        token_indices = jnp.sort(jax.random.randint(k4, (N_TRAIN,), 0, VOCAB, dtype=jnp.int32))
        return {'x': x, 'W': W, 'delta_values': delta_values, 'token_indices': token_indices}
    _L0_tok_all = _L0_tok_setup()
    _L0_tok_in = {k: v for k, v in _L0_tok_all.items() if k in ('W', 'delta_values', 'token_indices')}
    del _L0_tok_all

    def _L0_attn_setup():
        import jax, jax.numpy as jnp
        import numpy as np
        D_MODEL = 512
        NUM_HEADS = 32
        NUM_KV_HEADS = 8
        HEAD_DIM = D_MODEL // NUM_HEADS
        KV_GROUPS = NUM_HEADS // NUM_KV_HEADS
        key = jax.random.key(seed)
        k1, k2, k3, k4, k5 = jax.random.split(key, 5)
        scale = 0.02
        h_bsd = jax.random.normal(k1, (2, 512, D_MODEL), dtype=jnp.float32)
        w_q = jax.random.normal(k2, (NUM_HEADS * HEAD_DIM, D_MODEL), dtype=jnp.float32) * scale
        w_k = jax.random.normal(k3, (NUM_KV_HEADS * HEAD_DIM, D_MODEL), dtype=jnp.float32) * scale
        w_v = jax.random.normal(k4, (NUM_KV_HEADS * HEAD_DIM, D_MODEL), dtype=jnp.float32) * scale
        w_o = jax.random.normal(k5, (D_MODEL, NUM_HEADS * HEAD_DIM), dtype=jnp.float32) * scale
        return {'h_bsd': h_bsd, 'w_q': w_q, 'w_k': w_k, 'w_v': w_v, 'w_o': w_o}
    _L0_attn_all = _L0_attn_setup()
    _L0_attn_in = {k: v for k, v in _L0_attn_all.items() if k in ('w_q', 'w_k', 'w_v', 'w_o')}
    del _L0_attn_all

    def _L0_ffn_setup():
        import jax, jax.numpy as jnp
        import numpy as np
        B, S, H = (2, 512, 512)
        E, K, I = (64, 8, 192)

        def _moe_forward(hidden_states, gate_weight, w_gate, w_up, w_down):
            b, s, h = hidden_states.shape
            x = hidden_states.reshape(-1, h)
            logits = x.astype(jnp.float32) @ gate_weight.astype(jnp.float32).T
            scores = jax.nn.softmax(logits, axis=-1)
            topk_w, topk_idx = jax.lax.top_k(scores, K)
            topk_w = topk_w / jnp.sum(topk_w, axis=-1, keepdims=True)
            flat_ids = topk_idx.reshape(-1)
            expanded = jnp.repeat(x, K, axis=0)
            order = jnp.argsort(flat_ids)
            sorted_tokens = expanded[order]
            group_sizes = jnp.zeros((E,), jnp.int32).at[flat_ids].add(1)
            g = jax.lax.ragged_dot(sorted_tokens, w_gate, group_sizes)
            u = jax.lax.ragged_dot(sorted_tokens, w_up, group_sizes)
            out = jax.lax.ragged_dot(jax.nn.silu(g) * u, w_down, group_sizes)
            inv = jnp.argsort(order)
            outs = out[inv].reshape(-1, K, h)
            y = jnp.sum(outs * topk_w[:, :, None], axis=1)
            return y.reshape(b, s, h)
        key = jax.random.key(seed)
        k0, k1, k2, k3, k4 = jax.random.split(key, 5)
        hidden_states = jax.random.normal(k0, (B, S, H), dtype=jnp.float32)
        gate_weight = jax.random.normal(k1, (E, H), dtype=jnp.float32) * 0.02
        w_gate = jax.random.normal(k2, (E, H, I), dtype=jnp.float32) * 0.02
        w_up = jax.random.normal(k3, (E, H, I), dtype=jnp.float32) * 0.02
        w_down = jax.random.normal(k4, (E, I, H), dtype=jnp.float32) * 0.02
        return {'hidden_states': hidden_states, 'gate_weight': gate_weight, 'w_gate': w_gate, 'w_up': w_up, 'w_down': w_down}
    _L0_ffn_all = _L0_ffn_setup()
    _L0_ffn_in = {k: v for k, v in _L0_ffn_all.items() if k in ('gate_weight', 'w_gate', 'w_up', 'w_down')}
    del _L0_ffn_all
    return {'x': x, 'L0_tok_W': _L0_tok_in['W'], 'L0_tok_delta_values': _L0_tok_in['delta_values'], 'L0_tok_token_indices': _L0_tok_in['token_indices'], 'L0_attn_w_q': _L0_attn_in['w_q'], 'L0_attn_w_k': _L0_attn_in['w_k'], 'L0_attn_w_v': _L0_attn_in['w_v'], 'L0_attn_w_o': _L0_attn_in['w_o'], 'L0_ffn_gate_weight': _L0_ffn_in['gate_weight'], 'L0_ffn_w_gate': _L0_ffn_in['w_gate'], 'L0_ffn_w_up': _L0_ffn_in['w_up'], 'L0_ffn_w_down': _L0_ffn_in['w_down']}

def reference(x, L0_tok_W, L0_tok_delta_values, L0_tok_token_indices, L0_attn_w_q, L0_attn_w_k, L0_attn_w_v, L0_attn_w_o, L0_ffn_gate_weight, L0_ffn_w_gate, L0_ffn_w_up, L0_ffn_w_down):
    import jax
    import jax.numpy as jnp

    def _L0_tok_ref(x, W, delta_values, token_indices):
        import jax, jax.numpy as jnp
        import numpy as np
        VOCAB = 32000
        EMBED = 512
        N_TRAIN = 64
        BATCH, SEQ = (4, 1024)
        delta = delta_values.reshape(EMBED, N_TRAIN).T
        W_eff = W.at[token_indices].add(delta)
        return W_eff[x]

    def _L0_attn_ref(h_bsd, w_q, w_k, w_v, w_o):
        import jax, jax.numpy as jnp
        import numpy as np
        D_MODEL = 512
        NUM_HEADS = 32
        NUM_KV_HEADS = 8
        HEAD_DIM = D_MODEL // NUM_HEADS
        KV_GROUPS = NUM_HEADS // NUM_KV_HEADS
        b, s, _ = h_bsd.shape
        q = (h_bsd @ w_q.T).reshape(b, s, NUM_HEADS, HEAD_DIM).transpose(0, 2, 1, 3)
        k = (h_bsd @ w_k.T).reshape(b, s, NUM_KV_HEADS, HEAD_DIM).transpose(0, 2, 1, 3)
        v = (h_bsd @ w_v.T).reshape(b, s, NUM_KV_HEADS, HEAD_DIM).transpose(0, 2, 1, 3)
        k = jnp.repeat(k, KV_GROUPS, axis=1)
        v = jnp.repeat(v, KV_GROUPS, axis=1)
        attn = jnp.einsum('bqsh,bqlh->bqsl', q, k) / jnp.sqrt(jnp.float32(HEAD_DIM))
        attn = jax.nn.softmax(attn, axis=-1)
        out = jnp.einsum('bqsl,bqlh->bqsh', attn, v)
        out = out.transpose(0, 2, 1, 3).reshape(b, s, D_MODEL)
        return out @ w_o.T

    def _L0_ffn_ref(hidden_states, gate_weight, w_gate, w_up, w_down):
        import jax, jax.numpy as jnp
        import numpy as np
        B, S, H = (2, 512, 512)
        E, K, I = (64, 8, 192)

        def _moe_forward(hidden_states, gate_weight, w_gate, w_up, w_down):
            b, s, h = hidden_states.shape
            x = hidden_states.reshape(-1, h)
            logits = x.astype(jnp.float32) @ gate_weight.astype(jnp.float32).T
            scores = jax.nn.softmax(logits, axis=-1)
            topk_w, topk_idx = jax.lax.top_k(scores, K)
            topk_w = topk_w / jnp.sum(topk_w, axis=-1, keepdims=True)
            flat_ids = topk_idx.reshape(-1)
            expanded = jnp.repeat(x, K, axis=0)
            order = jnp.argsort(flat_ids)
            sorted_tokens = expanded[order]
            group_sizes = jnp.zeros((E,), jnp.int32).at[flat_ids].add(1)
            g = jax.lax.ragged_dot(sorted_tokens, w_gate, group_sizes)
            u = jax.lax.ragged_dot(sorted_tokens, w_up, group_sizes)
            out = jax.lax.ragged_dot(jax.nn.silu(g) * u, w_down, group_sizes)
            inv = jnp.argsort(order)
            outs = out[inv].reshape(-1, K, h)
            y = jnp.sum(outs * topk_w[:, :, None], axis=1)
            return y.reshape(b, s, h)
        return _moe_forward(hidden_states, gate_weight, w_gate, w_up, w_down)
    h = _L0_tok_ref(x, L0_tok_W, L0_tok_delta_values, L0_tok_token_indices)
    h = h + _L0_attn_ref(_layernorm(h, axis=-1), L0_attn_w_q, L0_attn_w_k, L0_attn_w_v, L0_attn_w_o)
    h = h + _L0_ffn_ref(_layernorm(h, axis=-1), L0_ffn_gate_weight, L0_ffn_w_gate, L0_ffn_w_up, L0_ffn_w_down)
    return h

_drawn_inputs = setup_inputs


def setup_inputs(seed=0):
    import zlib

    import numpy as np

    out = dict(_drawn_inputs(seed))
    spreads = {}
    factors = {'L0_attn_w_q': 6.693,
     'L0_attn_w_k': 7.081,
     'L0_ffn_gate_weight': 5.315,
     'L0_ffn_w_gate': 5.357,
     'L0_ffn_w_up': 4.941,
     'L0_ffn_w_down': 5.065}
    for name, (base, spread) in spreads.items():
        noise = np.random.default_rng([zlib.crc32(name.encode()), seed]).standard_normal(out[name].shape)
        drawn = base * np.exp(spread * noise) if base else spread * noise
        out[name] = jnp.asarray(drawn.astype(out[name].dtype))
    for name, factor in factors.items():
        out[name] = (out[name] * factor).astype(out[name].dtype)
    return out
```

```python
from contextlib import ExitStack

import concourse.bass as bass
from concourse import mybir

P = 128
F32 = mybir.dt.float32
BF16 = mybir.dt.bfloat16
I32 = mybir.dt.int32
U32 = mybir.dt.uint32
ALU = mybir.AluOpType
ACT = mybir.ActivationFunctionType
X = mybir.AxisListType.X

EPS = 1e-5
MASK = float(2.0 ** 100)
FAR = float(2 ** 22)
SLOTS = 4


class Chain:

    def __init__(self, eng, sem):
        self.eng, self.sem, self.count = eng, sem, 0

    def mark(self, ins):
        ins.then_inc(self.sem, 1)
        self.count += 1

    def wait(self):
        self.eng.wait_ge(self.sem, self.count)

    def restart(self):
        self.wait()
        self.eng.sem_clear(self.sem)
        self.count = 0


def hold(eng, sem, value, held):
    eng.wait_ge(sem, value)
    eng.sem_inc(held, 1)


def dedup_moe_lm_tower(nc, x, tok_w, tok_delta, tok_idx, w_q, w_k, w_v, w_o, gate_w, w_gate, w_up, w_down, out):
    B, S = x.shape
    VOCAB, D = tok_w.shape
    NTRAIN = tok_idx.shape[0]
    KVD = w_k.shape[0]
    E, _, I = w_gate.shape
    TOPK = 8
    DH = 16
    H = D // DH
    G = KVD // DH
    R = H // G
    C = D // P
    IC, IP = 2, I // 2
    ROWS = B * S
    NCH = ROWS // P + 1
    HALVES = G // 4
    PAIRS = (ROWS * TOPK // P + E) // 2
    TILES = 2 * PAIRS + 8
    assert S == P and C == 4 and R == 4 and G == 8 and H * DH == D

    xn_dram = nc.dram_tensor("xn_rows", (ROWS + P, D), F32).ap()
    y_dram = nc.dram_tensor("y_rows", (ROWS + P, D), F32).ap()
    list_dram = nc.dram_tensor("expert_lists", (NCH * P * E, 2), I32).ap()
    list_rows = list_dram.rearrange("(c r e) t -> r c (e t)", r=P, e=E)

    with ExitStack() as ctx:
        def sb(name, shape, dt=F32):
            return ctx.enter_context(nc.sbuf_tensor(name, shape, dt))

        def sem(name):
            return ctx.enter_context(nc.semaphore(name))

        bank = [ctx.enter_context(nc.psum_tensor(f"bank{i}", [P, 512], F32)) for i in range(8)]

        ident = sb("ident", [P, P])
        earlier = sb("earlier", [P, P])
        earlier_b = sb("earlier_b", [P, P], BF16)
        upto = sb("upto", [P, P], BF16)
        later = sb("later", [P, P])
        ones = sb("ones", [P, P])
        ones_b = sb("ones_b", [P, P], BF16)
        col = sb("col", [P, 256])
        row = sb("row", [P, 1])
        tile_starts = sb("tile_starts", [P, 16])
        zeros = sb("zeros", [P, D])
        pad_list = sb("pad_list", [P, E, 2], I32)

        wq_nat = sb("wq_nat", [P, C, D])
        wo_nat = sb("wo_nat", [P, C, D])
        wkv_nat = sb("wkv_nat", [P, 2, D])
        gw_nat = sb("gw_nat", [E, D])
        delta_nat = sb("delta_nat", [P, C, NTRAIN])
        wqT = sb("wqT", [P, C, D])
        woT = sb("woT", [P, C, D])
        wkvT = sb("wkvT", [P, C, 2 * KVD])
        gwT = sb("gwT", [P, C, E])
        delta = sb("delta", [NTRAIN, D])

        ids_row_i = sb("ids_row_i", [P, ROWS], I32)
        ids_col_i = sb("ids_col_i", [P, B], I32)
        train_i = sb("train_i", [P, NTRAIN], I32)
        ids_col = sb("ids_col", [P, B])
        train = sb("train", [P, NTRAIN])
        scratch = sb("scratch", [P, ROWS])
        same = sb("same", [P, ROWS])
        times = sb("times", [P, B])
        seen = sb("seen", [P, B])
        first = sb("first", [P, B])
        rank_in_seq = sb("rank_in_seq", [P, B])
        distinct = sb("distinct", [P, B])
        keep = sb("keep", [P, B])
        fill = sb("fill", [P, B + 1])
        skips = sb("skips", [P, B])
        offset = sb("offset", [P, B])
        slot_of = sb("slot_of", [P, B])
        first_slot = sb("first_slot", [P, B])
        chosen = sb("chosen", [P, B])
        rep_slot = sb("rep_slot", [P, B], I32)
        attrs = sb("attrs", [P, B, 4], BF16)
        low = sb("low", [P, B], I32)
        high = sb("high", [P, B], I32)
        ntiles_i = sb("ntiles_i", [1, 1], I32)

        pick = sb("pick", [P, B, P], BF16)
        rec = sb("rec", [P, 4])
        id_f = sb("id_f", [P, 1])
        id_i = sb("id_i", [P, 1], I32)
        seq_is = sb("seq_is", [P, B])
        valid = sb("valid", [P, 1])
        trained = sb("trained", [P, P])
        trainedT = sb("trainedT", [NTRAIN, P])
        w_row = sb("w_row", [P, D])
        h = sb("h", [P, D])
        stats = sb("stats", [P, 6])
        mv = sb("mv", [P, 2])
        minus_half = sb("minus_half", [P, 1])
        var_eps = sb("var_eps", [P, 1])
        rstd = sb("rstd", [P, 1])
        xn = sb("xn", [P, D])
        xnT = sb("xnT", [P, C, P])
        q_pad = sb("q_pad", [P, HALVES, R, 4, 32])
        k_pad = sb("k_pad", [P, HALVES, 4, 32])
        v_aug = sb("v_aug", [P, G, DH + 1])
        qT = sb("qT", [P, HALVES, R, P])
        kT = sb("kT", [P, HALVES, P])
        negmax = sb("negmax", [P, G, R])
        probs = sb("probs", [P, 2, R, P])
        probsT = sb("probsT", [P, 2, R, P])
        rden = sb("rden", [P, H])
        attn = sb("attn", [P, H, DH])
        h2 = sb("h2", [P, D])
        lmax = sb("lmax", [P, 1])
        lexp = sb("lexp", [P, E])
        lsum = sb("lsum", [P, 1])
        lrec = sb("lrec", [P, 1])
        score = sb("score", [P, E])
        top = sb("top", [P, TOPK])
        top_i = sb("top_i", [P, TOPK], U32)
        top_f = sb("top_f", [P, TOPK])
        topsum = sb("topsum", [P, 1])
        toprec = sb("toprec", [P, 1])
        is_e = sb("is_e", [P, TOPK, E])
        picked = sb("picked", [P, TOPK, E])
        mask = sb("mask", [P, E])
        mask_b = sb("mask_b", [P, E], BF16)
        rank = sb("rank", [P, E])
        taken = sb("taken", [P, E])
        rank_k = sb("rank_k", [P, TOPK])
        far = sb("far", [P, 1])
        dest_f = sb("dest_f", [P, TOPK])
        dest = sb("dest", [P, TOPK], I32)
        list_rec = sb("list_rec", [P, TOPK, 2], I32)
        my_slot = sb("my_slot", [P, 1])

        lists = sb("lists", [P, NCH * E, 2], I32)
        count_e = sb("count_e", [E, 1])
        more = sb("more", [E, 16])
        tiles_e = sb("tiles_e", [E, 1])
        tiles_eb = sb("tiles_eb", [E, 1], BF16)
        upto_e = sb("upto_e", [E, 1])
        past = sb("past", [E, TILES], BF16)
        t_exp = sb("t_exp", [1, TILES])
        t_used = sb("t_used", [1, TILES])
        t_end = sb("t_end", [1, TILES])
        t_col = sb("t_col", [1, TILES])
        t_slot = sb("t_slot", [1, TILES], I32)
        total_i = sb("total_i", [1, 1], I32)
        tab_col = sb("tab_col", [1, TILES], I32)
        tab_exp = sb("tab_exp", [1, TILES], I32)
        tab_slot = sb("tab_slot", [1, TILES], I32)
        tab_upto = sb("tab_upto", [1, E], I32)
        tab_pairs = sb("tab_pairs", [1, 1], I32)

        wgu = sb("wgu", [P, SLOTS, 2, C * I])
        wdn = sb("wdn", [IP, SLOTS, IC * D])
        gidx = [sb(f"gidx{u}", [P, 1], I32) for u in range(2)]
        sidx = [sb(f"sidx{u}", [P, 1], I32) for u in range(2)]
        xg = [wo_nat[:, u, :].rearrange("p (a c) -> p a c", c=C) for u in range(2)]
        xgT = [wo_nat[:, 2 + u, :].rearrange("p (c t) -> p c t", c=C) for u in range(2)]
        y = [wkv_nat[:, u, :] for u in range(2)]
        final = [wq_nat[:, u, :] for u in range(4)]
        silu = sb("silu", [P, I])
        hid = [sb(f"hid{u}", [P, IP, IC]) for u in range(2)]
        hidT = [sb(f"hidT{u}", [IP, IC, P]) for u in range(2)]

        consts = sem("consts")
        ids_in = sem("ids_in")
        weights_in = sem("weights_in")
        pads_written = sem("pads_written")
        prep_psum = sem("prep_psum")
        prep_out = sem("prep_out")
        first_ready = sem("first_ready")
        ranks_psum = sem("ranks_psum")
        chosen_ready = sem("chosen_ready")
        reps_psum = sem("reps_psum")
        ntiles_ready = sem("ntiles_ready")
        reps_ready = sem("reps_ready")
        held = sem("held")
        dve_steps = sem("dve_steps")
        act_steps = sem("act_steps")
        pool_steps = sem("pool_steps")
        pick_ready = sem("pick_ready")
        rec_psum = sem("rec_psum")
        id_ready = sem("id_ready")
        row_gathered = sem("row_gathered")
        trained_ready = sem("trained_ready")
        trainedT_psum = sem("trainedT_psum")
        trainedT_ready = sem("trainedT_ready")
        delta_psum = sem("delta_psum")
        var_ready = sem("var_ready")
        rstd_ready = sem("rstd_ready")
        xn_ready = sem("xn_ready")
        xnT_psum = sem("xnT_psum")
        xnT_ready = sem("xnT_ready")
        qkv_psum = sem("qkv_psum")
        q_ready = sem("q_ready")
        kv_ready = sem("kv_ready")
        qkT_psum = sem("qkT_psum")
        qkT_ready = sem("qkT_ready")
        scores_psum = sem("scores_psum")
        max_ready = sem("max_ready")
        probs_ready = sem("probs_ready")
        probsT_psum = sem("probsT_psum")
        probsT_ready = sem("probsT_ready")
        attn_psum = sem("attn_psum")
        proj_psum = sem("proj_psum")
        logits_psum = sem("logits_psum")
        lmax_ready = sem("lmax_ready")
        lexp_ready = sem("lexp_ready")
        mask_ready = sem("mask_ready")
        rank_psum = sem("rank_psum")
        list_ready = sem("list_ready")
        rows_stored = sem("rows_stored")
        h2_ready = sem("h2_ready")
        h2_stored = sem("h2_stored")
        lists_scattered = sem("lists_scattered")
        lists_free = sem("lists_free")
        in_turn = sem("in_turn")
        y_free = sem("y_free")
        counts_psum = sem("counts_psum")
        tiles_ready = sem("tiles_ready")
        upto_psum = sem("upto_psum")
        past_ready = sem("past_ready")
        table_psum = sem("table_psum")
        table_ready = sem("table_ready")
        slot_in = [sem(f"slot_in{s}") for s in range(SLOTS)]
        expert_in = sem("expert_in")
        xg_in = [sem(f"xg_in{u}") for u in range(2)]
        xgT_psum = sem("xgT_psum")
        xgT_ready = sem("xgT_ready")
        gu_psum = sem("gu_psum")
        silu_ready = sem("silu_ready")
        hid_ready = sem("hid_ready")
        hidT_psum = sem("hidT_psum")
        hidT_ready = sem("hidT_ready")
        y_psum = sem("y_psum")
        y_ready = sem("y_ready")
        final_in = [sem(f"final_in{u}") for u in range(4)]
        final_out = [sem(f"final_out{u}") for u in range(4)]

        list_flat = list_dram
        gate_v = w_gate.rearrange("e (p c) i -> e p (c i)", c=C)
        up_v = w_up.rearrange("e (p c) i -> e p (c i)", c=C)
        down_v = w_down.rearrange("e (p c) n -> e p (c n)", c=IC)
        out_v = out

        PREP = 12
        block = ctx.enter_context(nc.Block())

        @block.sync
        def _(sp):
            sp.sem_inc(rows_stored, 16)
            sp.sem_inc(h2_stored, 16)
            sp.dma_start(ids_col_i[:, :], x.rearrange("b s -> s b"), allow_slow_non_contiguous=True).then_inc(ids_in, 16)
            sp.dma_start(ids_row_i[:, :], x.rearrange("(o b) s -> o (b s)", o=1).broadcast_to([P, ROWS])).then_inc(ids_in, 16)
            sp.dma_start(train_i[:, :], tok_idx.rearrange("(o n) -> o n", o=1).broadcast_to([P, NTRAIN])).then_inc(ids_in, 16)
            sp.dma_start(delta_nat[:, :, :], tok_delta.rearrange("(c p n) -> p c n", c=C, p=P)).then_inc(weights_in, 16)
            sp.dma_start(wq_nat[:, :, :], w_q.rearrange("(c p) d -> p c d", p=P)).then_inc(weights_in, 16)
            sp.dma_start(wkv_nat[:, 0, :], w_k).then_inc(weights_in, 16)
            sp.dma_start(wkv_nat[:, 1, :], w_v).then_inc(weights_in, 16)
            sp.dma_start(wo_nat[:, :, :], w_o.rearrange("(c p) d -> p c d", p=P)).then_inc(weights_in, 16)
            sp.dma_start(gw_nat[:, :], gate_w).then_inc(weights_in, 16)
            sp.wait_ge(consts, 1)
            sp.dma_start(list_rows, pad_list[:, :, :].rearrange("p e t -> p (e t)").unsqueeze(1)
                         .broadcast_to([P, NCH, 2 * E])).then_inc(pads_written, 16)
            for rows in (xn_dram, y_dram):
                sp.dma_start(rows.rearrange("(c p) d -> p c d", p=P), zeros[:, :].unsqueeze(1).broadcast_to([P, NCH, D])
                             ).then_inc(pads_written, 16)
            def load_expert(e, s):
                sp.dma_start(wgu[:, s, 0, :], gate_v[e]).then_inc(slot_in[s], 16)
                sp.dma_start(wgu[:, s, 1, :], up_v[e]).then_inc(slot_in[s], 16)
                sp.dma_start(wdn[:, s, :], down_v[e]).then_inc(slot_in[s], 16)

            for s in range(SLOTS):
                load_expert(s, s)
            sp.wait_ge(ntiles_ready, 1)
            ntiles = sp.value_load(ntiles_i[0:1, 0:1], min_val=1, max_val=B)
            sp.wait_ge(pads_written, 48)
            with sp.Fori(0, ntiles) as n:
                sp.wait_ge(h2_ready, n + 1)
                sp.dma_start(y_dram[bass.ts(n, P), :], h2[:, :]).then_inc(h2_stored, 16)
                sp.wait_ge(xn_ready, n * 3 + 3)
                sp.dma_start(xn_dram[bass.ts(n, P), :], xn[:, :]).then_inc(rows_stored, 16)
            def landed(turn, s):
                sp.wait_ge(slot_in[s], turn * 48)
                sp.sem_inc(expert_in, 1)

            sp.wait_ge(table_ready, 1)
            for s in range(2):
                landed(1, s)
            with sp.Fori(0, E // SLOTS - 1) as r:
                for s in range(SLOTS):
                    landed(r + 1 + (s + 2) // SLOTS, (s + 2) % SLOTS)
                    done = sp.value_load(tab_upto[0:1, bass.ds(r * SLOTS + s, 1)], min_val=1, max_val=TILES)
                    sp.wait_ge(y_psum, done)
                    load_expert((r + 1) * SLOTS + s, s)
            for s in range(2, SLOTS):
                landed(E // SLOTS, s)
            for b in range(B):
                sp.wait_ge(final_in[b % 4], 16 * (b // 4 + 1))
                sp.dma_start(out_v[b], final[b % 4]).then_inc(final_out[b % 4], 16)
            for u in range(4):
                sp.wait_ge(final_out[u], 16 * (B // 4))

        @block.gpsimd
        def _(pool):
            steps = Chain(pool, pool_steps)
            pool.sem_inc(lists_free, 1)
            pool.sem_inc(y_free, 1)
            iota = nc.gpsimd.iota
            kw = dict(allow_small_or_imprecise_dtypes=True)
            steps.mark(nc.gpsimd.memset(ones[:, :], 1.0))
            steps.mark(nc.gpsimd.memset(ones_b[:, :], 1.0))
            steps.mark(nc.gpsimd.memset(zeros[:, :], 0.0))
            steps.mark(nc.gpsimd.memset(pad_list[:, :, :], 0))
            steps.mark(nc.gpsimd.memset(taken[:, :], 0.0))
            steps.mark(nc.gpsimd.memset(trained[:, :], 0.0))
            steps.mark(nc.gpsimd.memset(minus_half[:, :], -0.5))
            steps.mark(iota(col[:, :], [[1, 256]], base=0, channel_multiplier=0, **kw))
            steps.mark(iota(row[:, :], [[1, 1]], base=0, channel_multiplier=1, **kw))
            steps.mark(iota(my_slot[:, :], [[1, 1]], base=0, channel_multiplier=1, **kw))
            steps.mark(iota(tile_starts[:, :], [[P, 16]], base=0, channel_multiplier=0, **kw))
            steps.wait()
            steps.mark(iota(pad_list[:, :, 0], [[0, E]], base=ROWS, channel_multiplier=1))
            steps.mark(nc.gpsimd.affine_select(out=ident[:, :], in_=ones[:, :], compare_op=ALU.is_equal, fill=0.0,
                                               base=0, pattern=[[-1, P]], channel_multiplier=1))
            steps.mark(nc.gpsimd.affine_select(out=earlier[:, :], in_=ones[:, :], compare_op=ALU.is_gt, fill=0.0,
                                               base=0, pattern=[[1, P]], channel_multiplier=-1))
            steps.mark(nc.gpsimd.affine_select(out=later[:, :], in_=ones[:, :], compare_op=ALU.is_gt, fill=0.0,
                                               base=0, pattern=[[-1, P]], channel_multiplier=1))
            steps.mark(nc.gpsimd.affine_select(out=earlier_b[:, :], in_=ones_b[:, :], compare_op=ALU.is_gt, fill=0.0,
                                               base=0, pattern=[[1, P]], channel_multiplier=-1))
            steps.mark(nc.gpsimd.affine_select(out=upto[:, :], in_=ones_b[:, :], compare_op=ALU.is_ge, fill=0.0,
                                               base=0, pattern=[[1, P]], channel_multiplier=-1))
            steps.wait()
            nc.gpsimd.memset(q_pad[:, :, :, :, :], 0.0).then_inc(consts, 1)

            pool.wait_ge(ntiles_ready, 1)
            ntiles = pool.value_load(ntiles_i[0:1, 0:1], min_val=1, max_val=B)
            with pool.Fori(0, ntiles) as n:
                hold(pool, id_ready, n + 1, held)
                nc.gpsimd.indirect_dma_start(w_row[:, :], None, tok_w, bass.IndirectOffsetOnAxis(ap=id_i[:, 0:1], axis=0),
                                             bounds_check=VOCAB - 1, oob_is_err=False).then_inc(row_gathered, 16)
                for k in range(2):
                    pool.wait_ge(var_ready, n * 2 + k + 1)
                    nc.gpsimd.tensor_tensor(rstd[:, :], var_eps[:, :], minus_half[:, :], ALU.pow).then_inc(rstd_ready, 1)
                hold(pool, list_ready, n + 1, held)
                pool.wait_ge(pads_written, 48)
                for k in range(TOPK):
                    nc.gpsimd.indirect_dma_start(list_flat, bass.IndirectOffsetOnAxis(ap=dest[:, k:k + 1], axis=0),
                                                 list_rec[:, k, :], None, bounds_check=NCH * P * E - 1,
                                                 oob_is_err=False).then_inc(lists_scattered, 16)
                pool.wait_ge(lists_scattered, n * (16 * TOPK) + 16 * TOPK)
                pool.sem_inc(lists_free, 1)
            pool.dma_start(lists[:, :, :].rearrange("p (c e) t -> p c (e t)", c=NCH), list_rows).then_inc(in_turn, 16)

            pool.wait_ge(table_ready, 1)
            pairs = pool.value_load(tab_pairs[0:1, 0:1], min_val=1, max_val=PAIRS)
            hold(pool, rows_stored, ntiles * 16 + 16, held)
            hold(pool, h2_stored, ntiles * 16 + 16, held)
            pool.wait_ge(in_turn, 16)

            def column(g):
                return pool.value_load(tab_col[0:1, bass.ds(g, 1)], min_val=0, max_val=NCH * E - 1)

            def gather(g, u):
                c = column(g)
                steps.mark(nc.gpsimd.tensor_copy(gidx[u][:, :], lists[:, bass.ds(c, 1), 0]))
                steps.wait()
                nc.gpsimd.indirect_dma_start(xg[u].rearrange("p a c -> p (a c)"), None, xn_dram,
                                             bass.IndirectOffsetOnAxis(ap=gidx[u][:, 0:1], axis=0),
                                             bounds_check=ROWS + P - 1, oob_is_err=False).then_inc(xg_in[u], 16)

            def scatter(g, u):
                c = column(g)
                steps.mark(nc.gpsimd.tensor_copy(sidx[u][:, :], lists[:, bass.ds(c, 1), 0]))
                steps.wait()
                nc.gpsimd.indirect_dma_start(y_dram, bass.IndirectOffsetOnAxis(ap=sidx[u][:, 0:1], axis=0), y[u],
                                             None, bounds_check=ROWS + P - 1, oob_is_err=True,
                                             compute_op=ALU.add).then_inc(in_turn, 16)

            gather(0, 0)
            gather(1, 1)
            pool.wait_ge(xgT_psum, 1)
            pool.wait_ge(xg_in[0], 16)
            gather(2, 0)
            steps.restart()
            with pool.Fori(0, pairs) as m:
                for u in range(2):
                    g = m * 2 + u
                    pool.wait_ge(xgT_psum, g + 2)
                    hold(pool, xg_in[1 - u], m * 16 + 16 + 16 * u, held)
                    gather(g + 3, 1 - u)
                    pool.wait_ge(y_ready, g + 3)
                    pool.wait_ge(in_turn, g * 16 + 16)
                    pool.sem_inc(y_free, 1)
                    scatter(g, u)
                steps.restart()
            hold(pool, in_turn, pairs * 32 + 16, held)
            for u in range(2):
                hold(pool, xg_in[u], pairs * 16 + 32 - 16 * u, held)
            pool.wait_ge(reps_ready, 1)
            for b in range(B):
                if b >= 4:
                    pool.wait_ge(final_out[b % 4], 16 * (b // 4))
                nc.gpsimd.indirect_dma_start(final[b % 4], None, y_dram,
                                             bass.IndirectOffsetOnAxis(ap=rep_slot[:, b:b + 1], axis=0),
                                             bounds_check=ROWS + P - 1, oob_is_err=False).then_inc(final_in[b % 4], 16)

        @block.scalar
        def _(act):
            steps = Chain(act, act_steps)
            outs = [delta[:, :]] + [wqT[:, c, :] for c in range(C)]
            outs += [wkvT[:, 2 * i:2 * i + 2, :].rearrange("p a b -> p (a b)") for i in range(2)]
            outs += [woT[:, c, :] for c in range(C)] + [gwT[:, :, :].rearrange("p c e -> p (c e)")]
            assert len(outs) == PREP
            for i, o in enumerate(outs):
                act.wait_ge(prep_psum, i + 1)
                nc.scalar.copy(o, bank[i % 4][0:o.shape[0], 0:o.shape[1]]).then_inc(prep_out, 1)

            act.wait_ge(ntiles_ready, 1)
            ntiles = act.value_load(ntiles_i[0:1, 0:1], min_val=1, max_val=B)
            with act.Fori(0, ntiles) as n:
                act.wait_ge(trainedT_psum, n + 1)
                nc.scalar.copy(trainedT[:, :], bank[7][0:NTRAIN, 128:256]).then_inc(trainedT_ready, 1)
                act.wait_ge(xnT_psum, n * 3 + 1)
                nc.scalar.copy(xnT[:, :, :].rearrange("p c t -> p (c t)"), bank[5][:, :]).then_inc(xnT_ready, 1)
                act.wait_ge(qkv_psum, n + 1)
                nc.scalar.mul(v_aug[:, :, 0:DH], bank[6][:, KVD:2 * KVD].rearrange("p (g d) -> p g d", d=DH), rec[:, 2:3])
                nc.scalar.mul(v_aug[:, :, DH], ones[:, 0:G], rec[:, 2:3])
                for f in range(HALVES):
                    last = nc.scalar.copy(k_pad[:, f, :, 0:DH], bank[6][:, f * 64:f * 64 + 64]
                                          .rearrange("p (i d) -> p i d", d=DH))
                last.then_inc(kv_ready, 1)
                act.wait_ge(qkT_psum, n + 1)
                nc.scalar.copy(kT[:, :, :].rearrange("p f t -> p (f t)"), bank[2][:, 0:2 * P])
                nc.scalar.copy(qT[:, 0, :, :].rearrange("p r t -> p (r t)"), bank[0][:, :]).then_inc(qkT_ready, 1)
                for g in range(G):
                    act.wait_ge(max_ready, n * G + g + 1)
                    if g >= 2:
                        act.wait_ge(probsT_psum, n * G + g - 1)
                    for r in range(R):
                        last = nc.scalar.activation(probs[:, g % 2, r, :], bank[g % 4][:, r * P:(r + 1) * P], ACT.Exp,
                                                    bias=negmax[:, g, r:r + 1])
                    last.then_inc(probs_ready, 1)
                act.wait_ge(xnT_psum, n * 3 + 2)
                nc.scalar.copy(xnT[:, :, :].rearrange("p c t -> p (c t)"), bank[4][:, :]).then_inc(xnT_ready, 1)
                act.wait_ge(xnT_psum, n * 3 + 3)
                nc.scalar.copy(xnT[:, :, :].rearrange("p c t -> p (c t)"), bank[4][:, :]).then_inc(xnT_ready, 1)
                act.wait_ge(lmax_ready, n + 1)
                nc.scalar.activation(lexp[:, :], bank[6][:, 0:E], ACT.Exp, bias=lmax[:, 0:1],
                                     accum_out=lsum[:, 0:1]).then_inc(lexp_ready, 1)

            act.wait_ge(table_ready, 1)
            pairs = act.value_load(tab_pairs[0:1, 0:1], min_val=1, max_val=PAIRS)

            def transposed_rows(g, u):
                act.wait_ge(xgT_psum, g + 1)
                nc.scalar.copy(xgT[u].rearrange("p c t -> p (c t)"), bank[u][:, :]).then_inc(xgT_ready, 1)

            def silu_gate(g, u, after=True):
                if after:
                    act.wait_ge(hid_ready, g)
                act.wait_ge(gu_psum, g + 1)
                nc.scalar.activation(silu[:, :], bank[2 + u][:, 0:I], ACT.Silu).then_inc(silu_ready, 1)

            transposed_rows(0, 0)
            transposed_rows(1, 1)
            silu_gate(0, 0, after=False)
            with act.Fori(0, pairs) as m:
                for u in range(2):
                    g = m * 2 + u
                    silu_gate(g + 1, 1 - u)
                    transposed_rows(g + 2, u)

        @block.vector
        def _(dve):
            steps = Chain(dve, dve_steps)
            dve.sem_inc(y_ready, 2)
            step, wait = steps.mark, steps.wait
            ts, tt, stt, red = (nc.vector.tensor_scalar, nc.vector.tensor_tensor, nc.vector.scalar_tensor_tensor,
                                nc.vector.tensor_reduce)
            dve.wait_ge(ids_in, 48)
            for raw, ids in ((ids_row_i, scratch), (ids_col_i, ids_col), (train_i, train)):
                step(ts(ids[:, :], raw[:, :], 0.0, float(VOCAB), ALU.is_lt, ALU.mult))
                wait()
                step(tt(ids[:, :], ids[:, :], raw[:, :], ALU.add))
                wait()
                if ids is not train:
                    step(ts(ids[:, :], ids[:, :], float(VOCAB - 1), 0.0, ALU.min, ALU.max))
                    wait()
            dve.wait_ge(consts, 1)
            same_v = same[:, :].rearrange("p (b j) -> p b j", b=B)
            ids_v = scratch[:, :].rearrange("p (b j) -> p b j", b=B)
            step(tt(same_v, ids_v, ids_col[:, :].unsqueeze(2).broadcast_to([P, B, S]), ALU.is_equal))
            wait()
            step(red(times[:, :], same_v, X, ALU.add))
            step(tt(ids_v, same_v, later[:, :].unsqueeze(1).broadcast_to([P, B, S]), ALU.mult))
            wait()
            step(nc.vector.tensor_copy(attrs[:, :, 2], times[:, :]))
            step(red(seen[:, :], ids_v, X, ALU.add))
            wait()
            ts(first[:, :], seen[:, :], 0.0, None, ALU.is_equal).then_inc(first_ready, 1)
            step(nc.vector.tensor_copy(ids_col_i[:, :], ids_col[:, :]))
            wait()
            step(ts(low[:, :], ids_col_i[:, :], 255, None, ALU.bitwise_and))
            step(ts(high[:, :], ids_col_i[:, :], 8, None, ALU.logical_shift_right))
            wait()
            step(nc.vector.tensor_copy(attrs[:, :, 0], high[:, :]))
            step(nc.vector.tensor_copy(attrs[:, :, 1], low[:, :]))
            step(ts(attrs[:, :, 3], col[:, 0:B], 1.0, None, ALU.add))
            dve.wait_ge(ranks_psum, 1)
            step(nc.vector.tensor_copy(rank_in_seq[:, :], bank[7][:, 0:B]))
            step(nc.vector.tensor_copy(distinct[:, :], bank[7][:, 64:64 + B]))
            step(nc.vector.memset(fill[:, 0:1], 0.0))
            wait()
            for b in range(B):
                step(ts(keep[:, b:b + 1], distinct[:, b:b + 1], fill[:, b:b + 1], float(P), ALU.add, ALU.is_le))
                wait()
                step(stt(out=fill[:, b + 1:b + 2], in0=fill[:, b:b + 1], scalar=keep[:, b:b + 1],
                         in1=distinct[:, b:b + 1], op0=ALU.mult, op1=ALU.add))
                wait()
            step(ts(keep[:, :], keep[:, :], -1.0, 1.0, ALU.mult, ALU.add))
            wait()
            step(nc.vector.tensor_tensor_scan(skips[:, :], keep[:, :], zeros[:, 0:B], 0.0, ALU.add, ALU.add))
            wait()
            ins = ts(ntiles_i[0:1, 0:1], skips[0:1, B - 1:B], 1.0, None, ALU.add)
            ins.then_inc(ntiles_ready, 1)
            step(stt(out=offset[:, :], in0=skips[:, :], scalar=float(P), in1=fill[:, 1:B + 1], op0=ALU.mult, op1=ALU.add))
            wait()
            step(tt(offset[:, :], offset[:, :], distinct[:, :], ALU.subtract))
            wait()
            step(tt(slot_of[:, :], offset[:, :], rank_in_seq[:, :], ALU.add))
            wait()
            tt(chosen[:, :], slot_of[:, :], first[:, :], ALU.mult).then_inc(chosen_ready, 1)
            step(stt(out=first_slot[:, :], in0=slot_of[:, :], scalar=1.0, in1=first[:, :], op0=ALU.add, op1=ALU.mult))
            wait()
            step(ts(first_slot[:, :], first_slot[:, :], -1.0, None, ALU.add))
            dve.wait_ge(reps_psum, 1)
            nc.vector.tensor_copy(rep_slot[:, :], bank[6][:, 0:B]).then_inc(reps_ready, 1)

            dve.wait_ge(ntiles_ready, 1)
            ntiles = dve.value_load(ntiles_i[0:1, 0:1], min_val=1, max_val=B)
            dve.wait_ge(prep_out, PREP)
            steps.restart()
            with dve.Fori(0, ntiles) as n:
                tt(pick[:, :, :], first_slot[:, :].unsqueeze(2).broadcast_to([P, B, P]),
                   col[:, 0:P].unsqueeze(1).broadcast_to([P, B, P]), ALU.is_equal).then_inc(pick_ready, 1)
                dve.wait_ge(pick_ready, n + 1)
                step(ts(first_slot[:, :], first_slot[:, :], -float(P), None, ALU.add))
                dve.wait_ge(rec_psum, n + 1)
                step(nc.vector.tensor_copy(rec[:, :], bank[7][:, 0:4]))
                wait()
                step(stt(out=id_f[:, :], in0=rec[:, 0:1], scalar=256.0, in1=rec[:, 1:2], op0=ALU.mult, op1=ALU.add))
                wait()
                nc.vector.tensor_copy(id_i[:, :], id_f[:, :]).then_inc(id_ready, 1)
                ts(trained[:, 0:NTRAIN], train[:, :], id_f[:, 0:1], None, ALU.is_equal).then_inc(trained_ready, 1)
                step(ts(seq_is[:, :], col[:, 1:B + 1], rec[:, 3:4], None, ALU.is_equal))
                step(ts(valid[:, :], rec[:, 2:3], 0.0, None, ALU.is_gt))
                wait()
                step(ts(k_pad[:, :, :, DH:32].rearrange("p f i d -> p (f i) d"),
                        seq_is[:, :].unsqueeze(1).broadcast_to([P, G, B]), -1.0, None, ALU.add))
                step(ts(q_pad[:, :, :, :, DH:32].rearrange("p f r i d -> p (f r i) d"),
                        seq_is[:, :].unsqueeze(1).broadcast_to([P, H, B]), MASK, None, ALU.mult))
                dve.wait_ge(row_gathered, n * 16 + 16)
                dve.wait_ge(delta_psum, n + 1)
                step(tt(h[:, :], w_row[:, :], bank[4][:, :], ALU.add))
                wait()

                def layernorm(src, k):
                    step(nc.vector.bn_stats(stats[:, :], src))
                    wait()
                    step(nc.vector.bn_aggr(mv[:, :], stats[:, :]))
                    wait()
                    ts(var_eps[:, :], mv[:, 1:2], EPS, None, ALU.add).then_inc(var_ready, 1)
                    dve.wait_ge(rstd_ready, n * 2 + k)
                    ts(xn[:, :], src, mv[:, 0:1], rstd[:, 0:1], ALU.subtract, ALU.mult).then_inc(xn_ready, 1)

                dve.wait_ge(rows_stored, n * 16 + 16)
                layernorm(h[:, :], 1)
                dve.wait_ge(qkv_psum, n + 1)
                for f in range(HALVES):
                    last = ts(q_pad[:, f, :, :, 0:DH], bank[4][:, f * 256:f * 256 + 256]
                              .rearrange("p (i r d) -> p r i d", r=R, d=DH), DH ** -0.5, None, ALU.mult)
                    if f == HALVES - 1:
                        last.then_inc(q_ready, 1)
                dve.wait_ge(qkT_psum, n + 1)
                nc.vector.tensor_copy(qT[:, 1, :, :].rearrange("p r t -> p (r t)"), bank[1][:, :]).then_inc(qkT_ready, 1)

                def row_max(g):
                    dve.wait_ge(scores_psum, n * G + g + 1)
                    step(red(negmax[:, g, :], bank[g % 4][:, :].rearrange("p (r k) -> p r k", r=R), X, ALU.max))
                    wait()
                    ts(negmax[:, g, :], negmax[:, g, :], -1.0, None, ALU.mult).then_inc(max_ready, 1)

                for g in range(3):
                    row_max(g)
                for g in range(G):
                    if g + 3 < G:
                        row_max(g + 3)
                    dve.wait_ge(probsT_psum, n * G + g + 1)
                    nc.vector.tensor_copy(probsT[:, g % 2, :, :].rearrange("p r t -> p (r t)"),
                                          bank[4 + g % 2][:, :]).then_inc(probsT_ready, 1)
                dve.wait_ge(attn_psum, n + 1)
                for f in range(HALVES):
                    o = bank[6 + f][:, 0:16 * 17].rearrange("p (h d) -> p h d", d=17)
                    step(nc.vector.reciprocal(rden[:, f * 16:f * 16 + 16], o[:, :, DH]))
                wait()
                for f in range(HALVES):
                    o = bank[6 + f][:, 0:16 * 17].rearrange("p (h d) -> p h d", d=17)
                    last = tt(attn[:, f * 16:f * 16 + 16, :], o[:, :, 0:DH],
                              rden[:, f * 16:f * 16 + 16].unsqueeze(2).broadcast_to([P, 16, DH]), ALU.mult)
                last.then_inc(xn_ready, 1)
                dve.wait_ge(proj_psum, n + 1)
                dve.wait_ge(h2_stored, n * 16 + 16)
                tt(h2[:, :], h[:, :], bank[5][:, :], ALU.add).then_inc(h2_ready, 1)
                dve.wait_ge(h2_ready, n + 1)
                layernorm(h2[:, :], 2)
                dve.wait_ge(logits_psum, n + 1)
                step(red(lmax[:, :], bank[6][:, 0:E], X, ALU.max))
                wait()
                ts(lmax[:, :], lmax[:, :], -1.0, None, ALU.mult).then_inc(lmax_ready, 1)
                dve.wait_ge(lexp_ready, n + 1)
                step(nc.vector.reciprocal(lrec[:, :], lsum[:, :]))
                wait()
                step(ts(score[:, :], lexp[:, :], lrec[:, 0:1], None, ALU.mult))
                wait()
                step(nc.vector.max(top[:, :], score[:, :]))
                wait()
                step(nc.vector.max_index(top_i[:, :], top[:, :], score[:, :]))
                step(red(topsum[:, :], top[:, :], X, ALU.add))
                wait()
                step(nc.vector.reciprocal(toprec[:, :], topsum[:, :]))
                step(nc.vector.tensor_copy(top_f[:, :], top_i[:, :]))
                wait()
                step(tt(is_e[:, :, :], col[:, 0:E].unsqueeze(1).broadcast_to([P, TOPK, E]),
                        top_f[:, :].unsqueeze(2).broadcast_to([P, TOPK, E]), ALU.is_equal))
                wait()
                step(red(mask[:, :], is_e[:, :, :].rearrange("p k e -> p e k"), X, ALU.add))
                wait()
                ts(mask_b[:, :], mask[:, :], valid[:, 0:1], None, ALU.mult).then_inc(mask_ready, 1)
                dve.wait_ge(rank_psum, n + 1)
                step(tt(rank[:, :], taken[:, :], bank[7][:, 0:E], ALU.add))
                wait()
                step(tt(taken[:, :], taken[:, :], bank[7][:, E:2 * E], ALU.add))
                step(tt(picked[:, :, :], is_e[:, :, :], rank[:, :].unsqueeze(1).broadcast_to([P, TOPK, E]), ALU.mult))
                step(ts(far[:, :], valid[:, :], -FAR, FAR, ALU.mult, ALU.add))
                wait()
                step(red(rank_k[:, :], picked[:, :, :], X, ALU.add))
                wait()
                step(stt(out=dest_f[:, :], in0=rank_k[:, :], scalar=float(E), in1=top_f[:, :], op0=ALU.mult, op1=ALU.add))
                wait()
                dve.wait_ge(lists_free, n + 1)
                step(ts(dest[:, :], dest_f[:, :], far[:, 0:1], None, ALU.add))
                step(nc.vector.tensor_copy(list_rec[:, :, 0], my_slot[:, :].broadcast_to([P, TOPK])))
                step(ts(list_rec[:, :, 1].bitcast(F32), top[:, :], toprec[:, 0:1], None, ALU.mult))
                wait()
                ts(my_slot[:, :], my_slot[:, :], float(P), None, ALU.add).then_inc(list_ready, 1)
                steps.restart()

            dve.wait_ge(counts_psum, 1)
            step(nc.vector.tensor_copy(count_e[:, :], bank[0][0:E, 0:1]))
            wait()
            step(ts(more[:, :], tile_starts[0:E, :], count_e[:, 0:1], None, ALU.is_lt))
            wait()
            step(red(tiles_e[:, :], more[:, :], X, ALU.add))
            wait()
            ts(tiles_eb[:, :], tiles_e[:, :], 1.0, None, ALU.max).then_inc(tiles_ready, 1)
            dve.wait_ge(upto_psum, 1)
            step(nc.vector.tensor_copy(upto_e[:, :], bank[1][0:E, 0:1]))
            wait()
            ts(past[:, :], col[0:E, 0:TILES], upto_e[:, 0:1], None, ALU.is_ge).then_inc(past_ready, 1)
            dve.wait_ge(table_psum, 1)
            step(nc.vector.tensor_copy(t_exp[:, :], bank[2][0:1, 0:TILES]))
            step(nc.vector.tensor_copy(t_used[:, :], bank[3][0:1, 0:TILES]))
            step(ts(total_i[:, :], bank[4][0:1, 0:1], 1.0, None, ALU.add))
            step(nc.vector.tensor_copy(tab_upto[:, :], bank[5][0:1, 0:E]))
            wait()
            step(ts(t_end[:, :], t_exp[:, :], float(E), None, ALU.is_ge))
            step(tt(t_col[:, :], col[0:1, 0:TILES], t_used[:, :], ALU.subtract))
            step(ts(tab_pairs[:, :], total_i[:, :], 1, None, ALU.logical_shift_right))
            wait()
            step(stt(out=t_col[:, :], in0=t_col[:, :], scalar=float(E), in1=t_exp[:, :], op0=ALU.mult, op1=ALU.add))
            step(ts(t_exp[:, :], t_exp[:, :], float(E - 1), None, ALU.min))
            wait()
            step(ts(t_used[:, :], t_end[:, :], -1.0, 1.0, ALU.mult, ALU.add))
            step(nc.vector.tensor_copy(t_slot[:, :], t_exp[:, :]))
            step(ts(tab_exp[:, :], t_exp[:, :], 1.0, None, ALU.add))
            wait()
            step(tt(t_col[:, :], t_col[:, :], t_used[:, :], ALU.mult))
            step(ts(tab_slot[:, :], t_slot[:, :], SLOTS - 1, None, ALU.bitwise_and))
            wait()
            stt(out=tab_col[:, :], in0=t_end[:, :], scalar=float((NCH - 1) * E), in1=t_col[:, :], op0=ALU.mult,
                op1=ALU.add).then_inc(table_ready, 1)
            dve.wait_ge(table_ready, 1)
            dve.wait_ge(in_turn, 16)
            pairs = dve.value_load(tab_pairs[0:1, 0:1], min_val=1, max_val=PAIRS)

            def gate(g, u):
                c = dve.value_load(tab_col[0:1, bass.ds(g, 1)], min_val=0, max_val=NCH * E - 1)
                dve.wait_ge(silu_ready, g + 1)
                stt(out=hid[u][:, :, :].rearrange("p a c -> p (a c)"), in0=bank[2 + u][:, I:2 * I],
                    scalar=lists[:, bass.ds(c, 1), 1].bitcast(F32), in1=silu[:, :], op0=ALU.mult,
                    op1=ALU.mult).then_inc(hid_ready, 1)

            gate(0, 0)
            steps.restart()
            with dve.Fori(0, pairs) as m:
                for u in range(2):
                    g = m * 2 + u
                    dve.wait_ge(hidT_psum, g + 1)
                    nc.vector.tensor_copy(hidT[u][:, :, :].rearrange("p c t -> p (c t)"),
                                          bank[4 + u][0:IP, 0:IC * P]).then_inc(hidT_ready, 1)
                    gate(g + 1, 1 - u)
                    dve.wait_ge(y_free, g + 1)
                    dve.wait_ge(y_psum, g + 1)
                    nc.vector.tensor_copy(y[u], bank[6 + u][:, :]).then_inc(y_ready, 1)
                steps.restart()

        @block.tensor
        def _(pe):
            mm, tr = nc.tensor.matmul, nc.tensor.transpose
            pe.wait_ge(consts, 1)
            groups = [[(delta_nat[:, c, :], NTRAIN, c * P) for c in range(C)]]
            groups += [[(wq_nat[:, r, c * P:(c + 1) * P], P, r * P) for r in range(C)] for c in range(C)]
            groups += [[(wkv_nat[:, s, c * P:(c + 1) * P], P, (c % 2) * 2 * P + s * P) for c in (2 * i, 2 * i + 1)
                        for s in range(2)] for i in range(2)]
            groups += [[(wo_nat[:, r, c * P:(c + 1) * P], P, r * P) for r in range(C)] for c in range(C)]
            groups += [[(gw_nat[:, c * P:(c + 1) * P], P, c * E) for c in range(C)]]
            pe.wait_ge(weights_in, 96)
            for i, pieces in enumerate(groups):
                if i >= 4:
                    pe.wait_ge(prep_out, i - 3)
                for src, rows, at in pieces:
                    k = src.shape[0]
                    last = tr(bank[i % 4][0:rows, at:at + k], src, ident[0:k, 0:k])
                last.then_inc(prep_psum, 1)
            pe.wait_ge(first_ready, 1)
            mm(bank[7][:, 0:B], earlier[:, :], first[:, :], start=True, stop=True)
            mm(bank[7][:, 64:64 + B], ones[:, :], first[:, :], start=True, stop=True).then_inc(ranks_psum, 1)
            pe.wait_ge(chosen_ready, 1)
            for b in range(B):
                last = mm(bank[6][:, b:b + 1], same[:, b * S:(b + 1) * S], chosen[:, b:b + 1], start=True, stop=True)
            last.then_inc(reps_psum, 1)

            pe.wait_ge(reps_ready, 1)
            pe.wait_ge(ntiles_ready, 1)
            ntiles = pe.value_load(ntiles_i[0:1, 0:1], min_val=1, max_val=B)
            pe.wait_ge(prep_out, PREP)
            with pe.Fori(0, ntiles) as n:
                pe.wait_ge(pick_ready, n + 1)
                for b in range(B):
                    last = mm(bank[7][:, 0:4], pick[:, b, :], attrs[:, b, :], start=(b == 0), stop=(b == B - 1))
                last.then_inc(rec_psum, 1)
                pe.wait_ge(trained_ready, n + 1)
                tr(bank[7][:, 128:256], trained[:, :], ident[:, :]).then_inc(trainedT_psum, 1)
                pe.wait_ge(trainedT_ready, n + 1)
                mm(bank[4][:, :], trainedT[:, :], delta[:, :], start=True, stop=True).then_inc(delta_psum, 1)

                def transpose_rows(src, dst, k):
                    pe.wait_ge(xn_ready, n * 3 + k)
                    for c in range(C):
                        last = tr(dst[:, c * P:(c + 1) * P], src[:, c * P:(c + 1) * P], ident[:, :])
                    last.then_inc(xnT_psum, 1)
                    pe.wait_ge(xnT_ready, n * 3 + k)

                transpose_rows(xn, bank[5], 1)
                for c in range(C):
                    mm(bank[4][:, :], xnT[:, c, :], wqT[:, c, :], start=(c == 0), stop=(c == C - 1))
                for c in range(C):
                    last = mm(bank[6][:, 0:2 * KVD], xnT[:, c, :], wkvT[:, c, :], start=(c == 0), stop=(c == C - 1))
                last.then_inc(qkv_psum, 1)
                pe.wait_ge(q_ready, n + 1)
                pe.wait_ge(kv_ready, n + 1)
                for f in range(HALVES):
                    for r in range(R):
                        tr(bank[f][:, r * P:(r + 1) * P], q_pad[:, f, r, :, :].rearrange("p i d -> p (i d)"), ident[:, :])
                    last = tr(bank[2][:, f * P:(f + 1) * P], k_pad[:, f, :, :].rearrange("p i d -> p (i d)"), ident[:, :])
                last.then_inc(qkT_psum, 1)
                pe.wait_ge(qkT_ready, n * 2 + 2)

                def scores(g):
                    f, at = g // 4, g % 4 * 32
                    for r in range(R):
                        last = mm(bank[g % 4][:, r * P:(r + 1) * P], qT[at:at + 32, f, r, :], kT[at:at + 32, f, :],
                                  start=True, stop=True)
                    last.then_inc(scores_psum, 1)

                def transpose_probs(g):
                    pe.wait_ge(probs_ready, n * G + g + 1)
                    for r in range(R):
                        last = tr(bank[4 + g % 2][:, r * P:(r + 1) * P], probs[:, g % 2, r, :], ident[:, :])
                    last.then_inc(probsT_psum, 1)

                for g in range(4):
                    scores(g)
                transpose_probs(0)
                for g in range(G):
                    if g + 4 < G:
                        scores(g + 4)
                    if g + 1 < G:
                        transpose_probs(g + 1)
                    pe.wait_ge(probsT_ready, n * G + g + 1)
                    for r in range(R):
                        hd = g % 4 * R + r
                        last = mm(bank[6 + g // 4][:, hd * 17:hd * 17 + 17], probsT[:, g % 2, r, :], v_aug[:, g, :],
                                  start=True, stop=True)
                last.then_inc(attn_psum, 1)
                transpose_rows(attn[:, :, :].rearrange("p h d -> p (h d)"), bank[4], 2)
                for c in range(C):
                    last = mm(bank[5][:, :], xnT[:, c, :], woT[:, c, :], start=(c == 0), stop=(c == C - 1))
                last.then_inc(proj_psum, 1)
                transpose_rows(xn, bank[4], 3)
                for c in range(C):
                    last = mm(bank[6][:, 0:E], xnT[:, c, :], gwT[:, c, :], start=(c == 0), stop=(c == C - 1))
                last.then_inc(logits_psum, 1)
                pe.wait_ge(mask_ready, n + 1)
                mm(bank[7][:, 0:E], earlier_b[:, :], mask_b[:, :], start=True, stop=True)
                mm(bank[7][:, E:2 * E], ones_b[:, :], mask_b[:, :], start=True, stop=True).then_inc(rank_psum, 1)

            hold(pe, list_ready, ntiles, held)
            tr(bank[0][0:E, 0:P], taken[:, :], ident[:, :]).then_inc(counts_psum, 1)
            pe.wait_ge(tiles_ready, 1)
            mm(bank[1][0:E, 0:1], upto[0:E, 0:E], tiles_eb[:, :], start=True, stop=True).then_inc(upto_psum, 1)
            pe.wait_ge(past_ready, 1)
            mm(bank[2][0:1, 0:TILES], ones_b[0:E, 0:1], past[:, :], start=True, stop=True)
            mm(bank[3][0:1, 0:TILES], tiles_eb[:, :], past[:, :], start=True, stop=True)
            mm(bank[4][0:1, 0:1], ones_b[0:E, 0:1], tiles_eb[:, :], start=True, stop=True)
            mm(bank[5][0:1, 0:E], tiles_eb[:, :], upto[0:E, 0:E], start=True, stop=True).then_inc(table_psum, 1)

            pe.wait_ge(table_ready, 1)
            pairs = pe.value_load(tab_pairs[0:1, 0:1], min_val=1, max_val=PAIRS)

            def transpose_gathered(g, u, turn):
                pe.wait_ge(xg_in[u], turn * 16)
                for c in range(C):
                    last = tr(bank[u][:, c * P:(c + 1) * P], xg[u][:, :, c], ident[:, :])
                last.then_inc(xgT_psum, 1)

            def gate_up(g, u):
                slot = pe.value_load(tab_slot[0:1, bass.ds(g, 1)], min_val=0, max_val=SLOTS - 1)
                need = pe.value_load(tab_exp[0:1, bass.ds(g, 1)], min_val=1, max_val=E)
                pe.wait_ge(expert_in, need)
                pe.wait_ge(xgT_ready, g + 1)
                for c in range(C):
                    last = mm(bank[2 + u][:, 0:2 * I], xgT[u][:, c, :],
                              wgu[:, bass.ds(slot, 1), :, c * I:(c + 1) * I].rearrange("p o w i -> p (o w) i"),
                              start=(c == 0), stop=(c == C - 1))
                last.then_inc(gu_psum, 1)

            transpose_gathered(0, 0, 1)
            transpose_gathered(1, 1, 1)
            gate_up(0, 0)
            with pe.Fori(0, pairs) as m:
                for u in range(2):
                    g = m * 2 + u
                    pe.wait_ge(hid_ready, g + 1)
                    for c in range(IC):
                        last = tr(bank[4 + u][0:IP, c * P:(c + 1) * P], hid[u][:, :, c], ident[:, :])
                    last.then_inc(hidT_psum, 1)
                    gate_up(g + 1, 1 - u)
                    transpose_gathered(g + 2, u, m + 2)
                    slot = pe.value_load(tab_slot[0:1, bass.ds(g, 1)], min_val=0, max_val=SLOTS - 1)
                    pe.wait_ge(hidT_ready, g + 1)
                    pe.wait_ge(y_ready, g + 1)
                    for c in range(IC):
                        last = mm(bank[6 + u][:, :], hidT[u][:, c, :],
                                  wdn[:, bass.ds(slot, 1), c * D:(c + 1) * D].rearrange("p o n -> p (o n)"),
                                  start=(c == 0), stop=(c == IC - 1))
                    last.then_inc(y_psum, 1)


_INS = ['x', 'L0_tok_W', 'L0_tok_delta_values', 'L0_tok_token_indices', 'L0_attn_w_q', 'L0_attn_w_k', 'L0_attn_w_v',
        'L0_attn_w_o', 'L0_ffn_gate_weight', 'L0_ffn_w_gate', 'L0_ffn_w_up', 'L0_ffn_w_down']
_OUTS = [((16, 128, 512), 'float32')]
build = dedup_moe_lm_tower


def kernel(**inputs):
    import numpy as _np
    import concourse.bacc as _bacc
    from concourse import mybir as _mybir
    from concourse.bass_utils import run_bass_kernel_spmd as _run

    nc = _bacc.Bacc("TRN2", target_bir_lowering=False, num_devices=1)
    arrays, args = {}, []
    for name in _INS:
        a = _np.ascontiguousarray(inputs[name])
        arrays[f"in_{name}_dram"] = a
        args.append(nc.dram_tensor(f"in_{name}_dram", a.shape, _mybir.dt.from_np(a.dtype), kind="ExternalInput").ap())
    for i, (shape, dtype) in enumerate(_OUTS):
        dt = _mybir.dt.from_np(_np.dtype(dtype))
        args.append(nc.dram_tensor(f"out_{i}_dram", shape, dt, kind="ExternalOutput").ap())
    dedup_moe_lm_tower(nc, *args)
    r = _run(nc, [arrays], core_ids=[0])
    return r.results[0]["out_0_dram"]
```

```python
from contextlib import ExitStack

import concourse.bass as bass
from concourse import mybir

P = 128
F32 = mybir.dt.float32
BF16 = mybir.dt.bfloat16
I32 = mybir.dt.int32
U32 = mybir.dt.uint32
ALU = mybir.AluOpType
ACT = mybir.ActivationFunctionType
X = mybir.AxisListType.X

EPS = 1e-5
MASK = float(2.0 ** 100)
FAR = float(2 ** 22)
SLOTS = 4


class Chain:

    def __init__(self, eng, sem):
        self.eng, self.sem, self.count = eng, sem, 0

    def mark(self, ins):
        ins.then_inc(self.sem, 1)
        self.count += 1

    def wait(self):
        self.eng.wait_ge(self.sem, self.count)

    def restart(self):
        self.wait()
        self.eng.sem_clear(self.sem)
        self.count = 0


def hold(eng, sem, value, held):
    eng.wait_ge(sem, value)
    eng.sem_inc(held, 1)


def dedup_moe_lm_tower(nc, x, tok_w, tok_delta, tok_idx, w_q, w_k, w_v, w_o, gate_w, w_gate, w_up, w_down, out):
    B, S = x.shape
    VOCAB, D = tok_w.shape
    NTRAIN = tok_idx.shape[0]
    KVD = w_k.shape[0]
    E, _, I = w_gate.shape
    TOPK = 8
    DH = 16
    H = D // DH
    G = KVD // DH
    R = H // G
    C = D // P
    IC, IP = 2, I // 2
    ROWS = B * S
    NCH = ROWS // P + 1
    HALVES = G // 4
    PAIRS = (ROWS * TOPK // P + E) // 2
    TILES = 2 * PAIRS + 8
    assert S == P and C == 4 and R == 4 and G == 8 and H * DH == D

    xn_dram = nc.dram_tensor("xn_rows", (ROWS + P, D), F32).ap()
    y_dram = nc.dram_tensor("y_rows", (ROWS + P, D), F32).ap()
    list_dram = nc.dram_tensor("expert_lists", (NCH * P * E, 2), I32).ap()
    list_rows = list_dram.rearrange("(c r e) t -> r c (e t)", r=P, e=E)

    with ExitStack() as ctx:
        def sb(name, shape, dt=F32):
            return ctx.enter_context(nc.sbuf_tensor(name, shape, dt))

        def sem(name):
            return ctx.enter_context(nc.semaphore(name))

        bank = [ctx.enter_context(nc.psum_tensor(f"bank{i}", [P, 512], F32)) for i in range(8)]

        ident = sb("ident", [P, P])
        earlier = sb("earlier", [P, P])
        earlier_b = sb("earlier_b", [P, P], BF16)
        upto = sb("upto", [P, P], BF16)
        later = sb("later", [P, P])
        ones = sb("ones", [P, P])
        ones_b = sb("ones_b", [P, P], BF16)
        col = sb("col", [P, 256])
        row = sb("row", [P, 1])
        tile_starts = sb("tile_starts", [P, 16])
        zeros = sb("zeros", [P, D])
        pad_list = sb("pad_list", [P, E, 2], I32)

        wq_nat = sb("wq_nat", [P, C, D])
        wo_nat = sb("wo_nat", [P, C, D])
        wkv_nat = sb("wkv_nat", [P, 2, D])
        gw_nat = sb("gw_nat", [E, D])
        delta_nat = sb("delta_nat", [P, C, NTRAIN])
        wqT = sb("wqT", [P, C, D])
        woT = sb("woT", [P, C, D])
        wkvT = sb("wkvT", [P, C, 2 * KVD])
        gwT = sb("gwT", [P, C, E])
        delta = sb("delta", [NTRAIN, D])

        ids_row_i = sb("ids_row_i", [P, ROWS], I32)
        ids_col_i = sb("ids_col_i", [P, B], I32)
        train_i = sb("train_i", [P, NTRAIN], I32)
        ids_col = sb("ids_col", [P, B])
        train = sb("train", [P, NTRAIN])
        scratch = sb("scratch", [P, ROWS])
        same = sb("same", [P, ROWS])
        times = sb("times", [P, B])
        seen = sb("seen", [P, B])
        first = sb("first", [P, B])
        rank_in_seq = sb("rank_in_seq", [P, B])
        distinct = sb("distinct", [P, B])
        keep = sb("keep", [P, B])
        fill = sb("fill", [P, B + 1])
        skips = sb("skips", [P, B])
        offset = sb("offset", [P, B])
        slot_of = sb("slot_of", [P, B])
        first_slot = sb("first_slot", [P, B])
        chosen = sb("chosen", [P, B])
        rep_slot = sb("rep_slot", [P, B], I32)
        attrs = sb("attrs", [P, B, 4], BF16)
        low = sb("low", [P, B], I32)
        high = sb("high", [P, B], I32)
        ntiles_i = sb("ntiles_i", [1, 1], I32)

        pick = sb("pick", [P, B, P], BF16)
        rec = sb("rec", [P, 4])
        id_f = sb("id_f", [P, 1])
        id_i = sb("id_i", [P, 1], I32)
        seq_is = sb("seq_is", [P, B])
        valid_next = sb("valid_next", [P, 1])
        valid_now = sb("valid_now", [P, 1])
        valid = sb("valid", [P, 1])
        trained = sb("trained", [P, P])
        trainedT = sb("trainedT", [NTRAIN, P])
        w_row = sb("w_row", [P, D])
        h = sb("h", [P, D])
        h_next = scratch[:, 0:D]
        xn1 = scratch[:, D:2 * D]
        xn1T = scratch[:, 2 * D:3 * D].rearrange("p (c t) -> p c t", c=C)
        stats = sb("stats", [P, 6])
        mv = sb("mv", [P, 2])
        minus_half = sb("minus_half", [P, 1])
        var_eps = sb("var_eps", [P, 1])
        rstd = sb("rstd", [P, 1])
        xn = sb("xn", [P, D])
        xnT = sb("xnT", [P, C, P])
        q_pad = sb("q_pad", [P, HALVES, R, 4, 32])
        k_pad = sb("k_pad", [P, HALVES, 4, 32])
        v_aug = sb("v_aug", [P, G, DH + 1])
        qT = sb("qT", [P, HALVES, R, P])
        kT = ids_row_i[:, 0:HALVES * 4 * P].bitcast(F32).rearrange("p (f i t) -> p f i t", f=HALVES, i=4)
        negmax = sb("negmax", [P, G, 4])
        probs = sb("probs", [P, 2, 4, P])
        probsT = sb("probsT", [P, 2, 4, P])
        rden = sb("rden", [P, H])
        attn = sb("attn", [P, H, DH])
        h2 = sb("h2", [P, D])
        lmax = sb("lmax", [P, 1])
        lexp = sb("lexp", [P, E])
        lsum = sb("lsum", [P, 1])
        lrec = sb("lrec", [P, 1])
        score = sb("score", [P, E])
        top = sb("top", [P, TOPK])
        top_i = sb("top_i", [P, TOPK], U32)
        top_f = sb("top_f", [P, TOPK])
        topsum = sb("topsum", [P, 1])
        toprec = sb("toprec", [P, 1])
        is_e = sb("is_e", [P, TOPK, E])
        picked = sb("picked", [P, TOPK, E])
        mask = sb("mask", [P, E])
        mask_b = sb("mask_b", [P, E], BF16)
        rank = sb("rank", [P, E])
        taken = sb("taken", [P, E])
        rank_k = sb("rank_k", [P, TOPK])
        far = sb("far", [P, 1])
        dest_f = sb("dest_f", [P, TOPK])
        dest = sb("dest", [P, TOPK], I32)
        list_rec = sb("list_rec", [P, TOPK, 2], I32)
        my_slot = sb("my_slot", [P, 1])

        lists = sb("lists", [P, NCH * E, 2], I32)
        count_e = sb("count_e", [E, 1])
        more = sb("more", [E, 16])
        tiles_e = sb("tiles_e", [E, 1])
        tiles_eb = sb("tiles_eb", [E, 1], BF16)
        upto_e = sb("upto_e", [E, 1])
        past = sb("past", [E, TILES], BF16)
        t_exp = sb("t_exp", [1, TILES])
        t_used = sb("t_used", [1, TILES])
        t_end = sb("t_end", [1, TILES])
        t_col = sb("t_col", [1, TILES])
        t_slot = sb("t_slot", [1, TILES], I32)
        total_i = sb("total_i", [1, 1], I32)
        tab_col = sb("tab_col", [1, TILES], I32)
        tab_exp = sb("tab_exp", [1, TILES], I32)
        tab_slot = sb("tab_slot", [1, TILES], I32)
        tab_upto = sb("tab_upto", [1, E], I32)
        tab_pairs = sb("tab_pairs", [1, 1], I32)

        wgu = sb("wgu", [P, SLOTS, 2, C * I])
        wdn = sb("wdn", [IP, SLOTS, IC * D])
        gidx = [sb(f"gidx{u}", [P, 1], I32) for u in range(2)]
        sidx = [sb(f"sidx{u}", [P, 1], I32) for u in range(2)]
        xg = [wo_nat[:, u, :].rearrange("p (a c) -> p a c", c=C) for u in range(2)]
        xgT = [wo_nat[:, 2 + u, :].rearrange("p (c t) -> p c t", c=C) for u in range(2)]
        y = [wkv_nat[:, u, :] for u in range(2)]
        final = [wq_nat[:, u, :] for u in range(4)]
        silu = sb("silu", [P, I])
        hid = [sb(f"hid{u}", [P, IP, IC]) for u in range(2)]
        hidT = [sb(f"hidT{u}", [IP, IC, P]) for u in range(2)]

        consts = sem("consts")
        ids_in = sem("ids_in")
        weights_in = sem("weights_in")
        pads_written = sem("pads_written")
        prep_psum = sem("prep_psum")
        prep_out = sem("prep_out")
        first_ready = sem("first_ready")
        ranks_psum = sem("ranks_psum")
        chosen_ready = sem("chosen_ready")
        reps_psum = sem("reps_psum")
        ntiles_ready = sem("ntiles_ready")
        reps_ready = sem("reps_ready")
        held = sem("held")
        dve_steps = sem("dve_steps")
        act_steps = sem("act_steps")
        pool_steps = sem("pool_steps")
        pick_ready = sem("pick_ready")
        rec_psum = sem("rec_psum")
        id_ready = sem("id_ready")
        row_gathered = sem("row_gathered")
        trained_ready = sem("trained_ready")
        trainedT_psum = sem("trainedT_psum")
        trainedT_ready = sem("trainedT_ready")
        delta_psum = sem("delta_psum")
        var_ready = sem("var_ready")
        rstd_ready = sem("rstd_ready")
        xn1_ready = sem("xn1_ready")
        xn1T_psum = sem("xn1T_psum")
        xn1T_ready = sem("xn1T_ready")
        q_psum = sem("q_psum")
        kv_psum = sem("kv_psum")
        q_ready = sem("q_ready")
        kv_ready = sem("kv_ready")
        h_ready = sem("h_ready")
        qkT_psum = sem("qkT_psum")
        qT_ready = sem("qT_ready")
        kT_ready = sem("kT_ready")
        scores_psum = sem("scores_psum")
        max_ready = sem("max_ready")
        probs_ready = sem("probs_ready")
        probsT_psum = sem("probsT_psum")
        probsT_dve = sem("probsT_dve")
        probsT_act = sem("probsT_act")
        attn_psum = sem("attn_psum")
        attn_ready = sem("attn_ready")
        attnT_psum = sem("attnT_psum")
        attnT_ready = sem("attnT_ready")
        proj_psum = sem("proj_psum")
        xn2_ready = sem("xn2_ready")
        xn2T_psum = sem("xn2T_psum")
        xn2T_ready = sem("xn2T_ready")
        logits_psum = sem("logits_psum")
        lmax_ready = sem("lmax_ready")
        lexp_ready = sem("lexp_ready")
        mask_ready = sem("mask_ready")
        rank_psum = sem("rank_psum")
        list_ready = sem("list_ready")
        rows_stored = sem("rows_stored")
        h2_ready = sem("h2_ready")
        h2_stored = sem("h2_stored")
        lists_scattered = sem("lists_scattered")
        lists_free = sem("lists_free")
        in_turn = sem("in_turn")
        y_free = sem("y_free")
        counts_psum = sem("counts_psum")
        tiles_ready = sem("tiles_ready")
        upto_psum = sem("upto_psum")
        past_ready = sem("past_ready")
        table_psum = sem("table_psum")
        table_ready = sem("table_ready")
        slot_in = [sem(f"slot_in{s}") for s in range(SLOTS)]
        expert_in = sem("expert_in")
        xg_in = [sem(f"xg_in{u}") for u in range(2)]
        xgT_psum = sem("xgT_psum")
        xgT_ready = sem("xgT_ready")
        gu_psum = sem("gu_psum")
        silu_ready = sem("silu_ready")
        hid_ready = sem("hid_ready")
        hidT_psum = sem("hidT_psum")
        hidT_ready = sem("hidT_ready")
        y_psum = sem("y_psum")
        y_ready = sem("y_ready")
        final_in = [sem(f"final_in{u}") for u in range(4)]
        final_out = [sem(f"final_out{u}") for u in range(4)]

        list_flat = list_dram
        gate_v = w_gate.rearrange("e (p c) i -> e p (c i)", c=C)
        up_v = w_up.rearrange("e (p c) i -> e p (c i)", c=C)
        down_v = w_down.rearrange("e (p c) n -> e p (c n)", c=IC)
        out_v = out

        BY_DVE = (0, 4)
        BY_ACT = tuple(g for g in range(G) if g not in BY_DVE)

        PREP = 12
        block = ctx.enter_context(nc.Block())

        @block.sync
        def _(sp):
            sp.sem_inc(rows_stored, 16)
            sp.sem_inc(h2_stored, 16)
            sp.dma_start(ids_col_i[:, :], x.rearrange("b s -> s b"), allow_slow_non_contiguous=True).then_inc(ids_in, 16)
            sp.dma_start(ids_row_i[:, :], x.rearrange("(o b) s -> o (b s)", o=1).broadcast_to([P, ROWS])).then_inc(ids_in, 16)
            sp.dma_start(train_i[:, :], tok_idx.rearrange("(o n) -> o n", o=1).broadcast_to([P, NTRAIN])).then_inc(ids_in, 16)
            sp.dma_start(delta_nat[:, :, :], tok_delta.rearrange("(c p n) -> p c n", c=C, p=P)).then_inc(weights_in, 16)
            sp.dma_start(wq_nat[:, :, :], w_q.rearrange("(c p) d -> p c d", p=P)).then_inc(weights_in, 16)
            sp.dma_start(wkv_nat[:, 0, :], w_k).then_inc(weights_in, 16)
            sp.dma_start(wkv_nat[:, 1, :], w_v).then_inc(weights_in, 16)
            sp.dma_start(wo_nat[:, :, :], w_o.rearrange("(c p) d -> p c d", p=P)).then_inc(weights_in, 16)
            sp.dma_start(gw_nat[:, :], gate_w).then_inc(weights_in, 16)
            sp.wait_ge(consts, 1)
            sp.dma_start(list_rows, pad_list[:, :, :].rearrange("p e t -> p (e t)").unsqueeze(1)
                         .broadcast_to([P, NCH, 2 * E])).then_inc(pads_written, 16)
            for rows in (xn_dram, y_dram):
                sp.dma_start(rows.rearrange("(c p) d -> p c d", p=P), zeros[:, :].unsqueeze(1).broadcast_to([P, NCH, D])
                             ).then_inc(pads_written, 16)
            def load_expert(e, s):
                sp.dma_start(wgu[:, s, 0, :], gate_v[e]).then_inc(slot_in[s], 16)
                sp.dma_start(wgu[:, s, 1, :], up_v[e]).then_inc(slot_in[s], 16)
                sp.dma_start(wdn[:, s, :], down_v[e]).then_inc(slot_in[s], 16)

            for s in range(SLOTS):
                load_expert(s, s)
            sp.wait_ge(ntiles_ready, 1)
            ntiles = sp.value_load(ntiles_i[0:1, 0:1], min_val=1, max_val=B)
            sp.wait_ge(pads_written, 48)
            with sp.Fori(0, ntiles) as n:
                sp.wait_ge(h2_ready, n + 1)
                sp.dma_start(y_dram[bass.ts(n, P), :], h2[:, :]).then_inc(h2_stored, 16)
                sp.wait_ge(xn2_ready, n + 1)
                sp.dma_start(xn_dram[bass.ts(n, P), :], xn[:, :]).then_inc(rows_stored, 16)
            def landed(turn, s):
                sp.wait_ge(slot_in[s], turn * 48)
                sp.sem_inc(expert_in, 1)

            sp.wait_ge(table_ready, 1)
            for s in range(2):
                landed(1, s)
            with sp.Fori(0, E // SLOTS - 1) as r:
                for s in range(SLOTS):
                    landed(r + 1 + (s + 2) // SLOTS, (s + 2) % SLOTS)
                    done = sp.value_load(tab_upto[0:1, bass.ds(r * SLOTS + s, 1)], min_val=1, max_val=TILES)
                    sp.wait_ge(y_psum, done)
                    load_expert((r + 1) * SLOTS + s, s)
            for s in range(2, SLOTS):
                landed(E // SLOTS, s)
            for b in range(B):
                sp.wait_ge(final_in[b % 4], 16 * (b // 4 + 1))
                sp.dma_start(out_v[b], final[b % 4]).then_inc(final_out[b % 4], 16)
            for u in range(4):
                sp.wait_ge(final_out[u], 16 * (B // 4))

        @block.gpsimd
        def _(pool):
            steps = Chain(pool, pool_steps)
            pool.sem_inc(lists_free, 1)
            pool.sem_inc(y_free, 1)
            iota = nc.gpsimd.iota
            kw = dict(allow_small_or_imprecise_dtypes=True)
            steps.mark(nc.gpsimd.memset(ones[:, :], 1.0))
            steps.mark(nc.gpsimd.memset(ones_b[:, :], 1.0))
            steps.mark(nc.gpsimd.memset(zeros[:, :], 0.0))
            steps.mark(nc.gpsimd.memset(pad_list[:, :, :], 0))
            steps.mark(nc.gpsimd.memset(taken[:, :], 0.0))
            steps.mark(nc.gpsimd.memset(trained[:, :], 0.0))
            steps.mark(nc.gpsimd.memset(minus_half[:, :], -0.5))
            for t in (valid_next, valid):
                steps.mark(nc.gpsimd.memset(t[:, :], 0.0))
            for t in (lexp, lsum):
                steps.mark(nc.gpsimd.memset(t[:, :], 1.0))
            steps.mark(iota(col[:, :], [[1, 256]], base=0, channel_multiplier=0, **kw))
            steps.mark(iota(row[:, :], [[1, 1]], base=0, channel_multiplier=1, **kw))
            steps.mark(iota(my_slot[:, :], [[1, 1]], base=-P, channel_multiplier=1, **kw))
            steps.mark(iota(tile_starts[:, :], [[P, 16]], base=0, channel_multiplier=0, **kw))
            steps.wait()
            steps.mark(iota(pad_list[:, :, 0], [[0, E]], base=ROWS, channel_multiplier=1))
            steps.mark(nc.gpsimd.affine_select(out=ident[:, :], in_=ones[:, :], compare_op=ALU.is_equal, fill=0.0,
                                               base=0, pattern=[[-1, P]], channel_multiplier=1))
            steps.mark(nc.gpsimd.affine_select(out=earlier[:, :], in_=ones[:, :], compare_op=ALU.is_gt, fill=0.0,
                                               base=0, pattern=[[1, P]], channel_multiplier=-1))
            steps.mark(nc.gpsimd.affine_select(out=later[:, :], in_=ones[:, :], compare_op=ALU.is_gt, fill=0.0,
                                               base=0, pattern=[[-1, P]], channel_multiplier=1))
            steps.mark(nc.gpsimd.affine_select(out=earlier_b[:, :], in_=ones_b[:, :], compare_op=ALU.is_gt, fill=0.0,
                                               base=0, pattern=[[1, P]], channel_multiplier=-1))
            steps.mark(nc.gpsimd.affine_select(out=upto[:, :], in_=ones_b[:, :], compare_op=ALU.is_ge, fill=0.0,
                                               base=0, pattern=[[1, P]], channel_multiplier=-1))
            steps.wait()
            nc.gpsimd.memset(q_pad[:, :, :, :, :], 0.0).then_inc(consts, 1)

            pool.wait_ge(ntiles_ready, 1)
            ntiles = pool.value_load(ntiles_i[0:1, 0:1], min_val=1, max_val=B)

            def gather_rows(t):
                hold(pool, id_ready, t + 1, held)
                nc.gpsimd.indirect_dma_start(w_row[:, :], None, tok_w, bass.IndirectOffsetOnAxis(ap=id_i[:, 0:1], axis=0),
                                             bounds_check=VOCAB - 1, oob_is_err=False).then_inc(row_gathered, 16)

            def inverse_root(k):
                pool.wait_ge(var_ready, k)
                nc.gpsimd.tensor_tensor(rstd[:, :], var_eps[:, :], minus_half[:, :], ALU.pow).then_inc(rstd_ready, 1)

            def scatter_lists(ks):
                for k in ks:
                    nc.gpsimd.indirect_dma_start(list_flat, bass.IndirectOffsetOnAxis(ap=dest[:, k:k + 1], axis=0),
                                                 list_rec[:, k, :], None, bounds_check=NCH * P * E - 1,
                                                 oob_is_err=False).then_inc(lists_scattered, 16)

            def lists_done(k):
                pool.wait_ge(lists_scattered, k * (16 * TOPK) + 16 * TOPK)
                pool.sem_inc(lists_free, 1)

            gather_rows(0)
            inverse_root(1)
            pool.wait_ge(pads_written, 48)
            with pool.Fori(0, ntiles) as n:
                gather_rows(n + 1)
                inverse_root(n * 2 + 2)
                hold(pool, list_ready, n + 1, held)
                scatter_lists(range(TOPK))
                lists_done(n)
                inverse_root(n * 2 + 3)
            hold(pool, list_ready, ntiles + 1, held)
            scatter_lists(range(TOPK))
            lists_done(ntiles)
            pool.dma_start(lists[:, :, :].rearrange("p (c e) t -> p c (e t)", c=NCH), list_rows).then_inc(in_turn, 16)

            pool.wait_ge(table_ready, 1)
            pairs = pool.value_load(tab_pairs[0:1, 0:1], min_val=1, max_val=PAIRS)
            hold(pool, rows_stored, ntiles * 16 + 16, held)
            hold(pool, h2_stored, ntiles * 16 + 16, held)
            pool.wait_ge(in_turn, 16)

            def column(g):
                return pool.value_load(tab_col[0:1, bass.ds(g, 1)], min_val=0, max_val=NCH * E - 1)

            def gather(g, u):
                c = column(g)
                steps.mark(nc.gpsimd.tensor_copy(gidx[u][:, :], lists[:, bass.ds(c, 1), 0]))
                steps.wait()
                nc.gpsimd.indirect_dma_start(xg[u].rearrange("p a c -> p (a c)"), None, xn_dram,
                                             bass.IndirectOffsetOnAxis(ap=gidx[u][:, 0:1], axis=0),
                                             bounds_check=ROWS + P - 1, oob_is_err=False).then_inc(xg_in[u], 16)

            def scatter(g, u):
                c = column(g)
                steps.mark(nc.gpsimd.tensor_copy(sidx[u][:, :], lists[:, bass.ds(c, 1), 0]))
                steps.wait()
                nc.gpsimd.indirect_dma_start(y_dram, bass.IndirectOffsetOnAxis(ap=sidx[u][:, 0:1], axis=0), y[u],
                                             None, bounds_check=ROWS + P - 1, oob_is_err=True,
                                             compute_op=ALU.add).then_inc(in_turn, 16)

            gather(0, 0)
            gather(1, 1)
            pool.wait_ge(xgT_psum, 1)
            pool.wait_ge(xg_in[0], 16)
            gather(2, 0)
            steps.restart()
            with pool.Fori(0, pairs) as m:
                for u in range(2):
                    g = m * 2 + u
                    pool.wait_ge(xgT_psum, g + 2)
                    hold(pool, xg_in[1 - u], m * 16 + 16 + 16 * u, held)
                    gather(g + 3, 1 - u)
                    pool.wait_ge(y_ready, g + 3)
                    pool.wait_ge(in_turn, g * 16 + 16)
                    pool.sem_inc(y_free, 1)
                    scatter(g, u)
                steps.restart()
            hold(pool, in_turn, pairs * 32 + 16, held)
            for u in range(2):
                hold(pool, xg_in[u], pairs * 16 + 32 - 16 * u, held)
            pool.wait_ge(reps_ready, 1)
            for b in range(B):
                if b >= 4:
                    pool.wait_ge(final_out[b % 4], 16 * (b // 4))
                nc.gpsimd.indirect_dma_start(final[b % 4], None, y_dram,
                                             bass.IndirectOffsetOnAxis(ap=rep_slot[:, b:b + 1], axis=0),
                                             bounds_check=ROWS + P - 1, oob_is_err=False).then_inc(final_in[b % 4], 16)

        @block.scalar
        def _(act):
            steps = Chain(act, act_steps)
            act.sem_inc(lexp_ready, 1)
            outs = [delta[:, :]] + [wqT[:, c, :] for c in range(C)]
            outs += [wkvT[:, 2 * i:2 * i + 2, :].rearrange("p a b -> p (a b)") for i in range(2)]
            outs += [woT[:, c, :] for c in range(C)] + [gwT[:, :, :].rearrange("p c e -> p (c e)")]
            assert len(outs) == PREP
            for i, o in enumerate(outs):
                act.wait_ge(prep_psum, i + 1)
                nc.scalar.copy(o, bank[i % 4][0:o.shape[0], 0:o.shape[1]]).then_inc(prep_out, 1)

            act.wait_ge(ntiles_ready, 1)
            ntiles = act.value_load(ntiles_i[0:1, 0:1], min_val=1, max_val=B)

            def embed_delta(t):
                act.wait_ge(trainedT_psum, t + 1)
                nc.scalar.copy(trainedT[:, :], bank[3][0:NTRAIN, 128:256]).then_inc(trainedT_ready, 1)

            def embed_transposed(t):
                act.wait_ge(xn1T_psum, t + 1)
                nc.scalar.copy(xn1T.rearrange("p c t -> p (c t)"), bank[3][:, :]).then_inc(xn1T_ready, 1)

            def queries(t):
                act.wait_ge(q_psum, t + 1)
                for f in range(HALVES):
                    last = nc.scalar.mul(q_pad[:, f, :, :, 0:DH], bank[2][:, f * 256:f * 256 + 256]
                                         .rearrange("p (i r d) -> p r i d", r=R, d=DH), DH ** -0.5)
                last.then_inc(q_ready, 1)

            def keys_values(t):
                act.wait_ge(kv_psum, t + 1)
                nc.scalar.mul(v_aug[:, :, 0:DH], bank[0][:, KVD:2 * KVD].rearrange("p (g d) -> p g d", d=DH), rec[:, 2:3])
                nc.scalar.mul(v_aug[:, :, DH], ones[:, 0:G], rec[:, 2:3])
                for f in range(HALVES):
                    last = nc.scalar.copy(k_pad[:, f, :, 0:DH], bank[0][:, f * 64:f * 64 + 64]
                                          .rearrange("p (i d) -> p i d", d=DH))
                last.then_inc(kv_ready, 1)

            def transposed_queries(t):
                act.wait_ge(qkT_psum, t + 1)
                for f in range(HALVES):
                    nc.scalar.copy(qT[:, f, :, :].rearrange("p r t -> p (r t)"), bank[f][:, :]).then_inc(qT_ready, 1)
                nc.scalar.copy(h[:, :], h_next).then_inc(h_ready, 1)

            def transposed_probs(n, g):
                act.wait_ge(probsT_psum, n * G + g + 1)
                nc.scalar.copy(probsT[:, g % 2, :, :].rearrange("p r t -> p (r t)"), bank[4 + g % 2][:, :]
                               ).then_inc(probsT_act, 1)

            embed_delta(0)
            embed_transposed(0)
            queries(0)
            keys_values(0)
            transposed_queries(0)
            with act.Fori(0, ntiles) as n:
                for g in range(G):
                    act.wait_ge(max_ready, n * G + g + 1)
                    if g >= 2:
                        act.wait_ge(probsT_psum, n * G + g - 1)
                    for i in range(4):
                        last = nc.scalar.activation(probs[:, g % 2, i, :], bank[g % 3][:, i * P:(i + 1) * P], ACT.Exp,
                                                    bias=negmax[:, g, i:i + 1])
                    last.then_inc(probs_ready, 1)
                    if g == 0:
                        embed_delta(n + 1)
                    if g - 1 in BY_ACT:
                        transposed_probs(n, g - 1)
                transposed_probs(n, G - 1)
                embed_transposed(n + 1)
                act.wait_ge(attnT_psum, n + 1)
                nc.scalar.copy(xnT[:, :, :].rearrange("p c t -> p (c t)"), bank[4][:, :]).then_inc(attnT_ready, 1)
                queries(n + 1)
                keys_values(n + 1)
                act.wait_ge(xn2T_psum, n + 1)
                nc.scalar.copy(xnT[:, :, :].rearrange("p c t -> p (c t)"), bank[4][:, :]).then_inc(xn2T_ready, 1)
                transposed_queries(n + 1)
                act.wait_ge(lmax_ready, n + 1)
                nc.scalar.activation(lexp[:, :], bank[5][:, 0:E], ACT.Exp, bias=lmax[:, 0:1],
                                     accum_out=lsum[:, 0:1]).then_inc(lexp_ready, 1)

            act.wait_ge(table_ready, 1)
            pairs = act.value_load(tab_pairs[0:1, 0:1], min_val=1, max_val=PAIRS)

            def transposed_rows(g, u):
                act.wait_ge(xgT_psum, g + 1)
                nc.scalar.copy(xgT[u].rearrange("p c t -> p (c t)"), bank[u][:, :]).then_inc(xgT_ready, 1)

            def silu_gate(g, u, after=True):
                if after:
                    act.wait_ge(hid_ready, g)
                act.wait_ge(gu_psum, g + 1)
                nc.scalar.activation(silu[:, :], bank[2 + u][:, 0:I], ACT.Silu).then_inc(silu_ready, 1)

            transposed_rows(0, 0)
            transposed_rows(1, 1)
            silu_gate(0, 0, after=False)
            with act.Fori(0, pairs) as m:
                for u in range(2):
                    g = m * 2 + u
                    silu_gate(g + 1, 1 - u)
                    transposed_rows(g + 2, u)

        @block.vector
        def _(dve):
            steps = Chain(dve, dve_steps)
            dve.sem_inc(y_ready, 2)
            step, wait = steps.mark, steps.wait
            ts, tt, stt, red = (nc.vector.tensor_scalar, nc.vector.tensor_tensor, nc.vector.scalar_tensor_tensor,
                                nc.vector.tensor_reduce)
            dve.wait_ge(ids_in, 48)
            for raw, ids in ((ids_row_i, scratch), (ids_col_i, ids_col), (train_i, train)):
                step(ts(ids[:, :], raw[:, :], 0.0, float(VOCAB), ALU.is_lt, ALU.mult))
                wait()
                step(tt(ids[:, :], ids[:, :], raw[:, :], ALU.add))
                wait()
                if ids is not train:
                    step(ts(ids[:, :], ids[:, :], float(VOCAB - 1), 0.0, ALU.min, ALU.max))
                    wait()
            dve.wait_ge(consts, 1)
            same_v = same[:, :].rearrange("p (b j) -> p b j", b=B)
            ids_v = scratch[:, :].rearrange("p (b j) -> p b j", b=B)
            step(tt(same_v, ids_v, ids_col[:, :].unsqueeze(2).broadcast_to([P, B, S]), ALU.is_equal))
            wait()
            step(red(times[:, :], same_v, X, ALU.add))
            step(tt(ids_v, same_v, later[:, :].unsqueeze(1).broadcast_to([P, B, S]), ALU.mult))
            wait()
            step(nc.vector.tensor_copy(attrs[:, :, 2], times[:, :]))
            step(red(seen[:, :], ids_v, X, ALU.add))
            wait()
            ts(first[:, :], seen[:, :], 0.0, None, ALU.is_equal).then_inc(first_ready, 1)
            step(nc.vector.tensor_copy(ids_col_i[:, :], ids_col[:, :]))
            wait()
            step(ts(low[:, :], ids_col_i[:, :], 255, None, ALU.bitwise_and))
            step(ts(high[:, :], ids_col_i[:, :], 8, None, ALU.logical_shift_right))
            wait()
            step(nc.vector.tensor_copy(attrs[:, :, 0], high[:, :]))
            step(nc.vector.tensor_copy(attrs[:, :, 1], low[:, :]))
            step(ts(attrs[:, :, 3], col[:, 0:B], 1.0, None, ALU.add))
            step(nc.vector.memset(kT, 0.0))
            dve.wait_ge(ranks_psum, 1)
            step(nc.vector.tensor_copy(rank_in_seq[:, :], bank[7][:, 0:B]))
            step(nc.vector.tensor_copy(distinct[:, :], bank[7][:, 64:64 + B]))
            step(nc.vector.memset(fill[:, 0:1], 0.0))
            wait()
            for b in range(B):
                step(ts(keep[:, b:b + 1], distinct[:, b:b + 1], fill[:, b:b + 1], float(P), ALU.add, ALU.is_le))
                wait()
                step(stt(out=fill[:, b + 1:b + 2], in0=fill[:, b:b + 1], scalar=keep[:, b:b + 1],
                         in1=distinct[:, b:b + 1], op0=ALU.mult, op1=ALU.add))
                wait()
            step(ts(keep[:, :], keep[:, :], -1.0, 1.0, ALU.mult, ALU.add))
            wait()
            step(nc.vector.tensor_tensor_scan(skips[:, :], keep[:, :], zeros[:, 0:B], 0.0, ALU.add, ALU.add))
            wait()
            ins = ts(ntiles_i[0:1, 0:1], skips[0:1, B - 1:B], 1.0, None, ALU.add)
            ins.then_inc(ntiles_ready, 1)
            step(stt(out=offset[:, :], in0=skips[:, :], scalar=float(P), in1=fill[:, 1:B + 1], op0=ALU.mult, op1=ALU.add))
            wait()
            step(tt(offset[:, :], offset[:, :], distinct[:, :], ALU.subtract))
            wait()
            step(tt(slot_of[:, :], offset[:, :], rank_in_seq[:, :], ALU.add))
            wait()
            tt(chosen[:, :], slot_of[:, :], first[:, :], ALU.mult).then_inc(chosen_ready, 1)
            step(stt(out=first_slot[:, :], in0=slot_of[:, :], scalar=1.0, in1=first[:, :], op0=ALU.add, op1=ALU.mult))
            wait()
            step(ts(first_slot[:, :], first_slot[:, :], -1.0, None, ALU.add))
            dve.wait_ge(ntiles_ready, 1)
            ntiles = dve.value_load(ntiles_i[0:1, 0:1], min_val=1, max_val=B)
            dve.wait_ge(prep_out, PREP)
            steps.restart()

            def pick_tokens(t):
                tt(pick[:, :, :], first_slot[:, :].unsqueeze(2).broadcast_to([P, B, P]),
                   col[:, 0:P].unsqueeze(1).broadcast_to([P, B, P]), ALU.is_equal).then_inc(pick_ready, 1)
                dve.wait_ge(pick_ready, t + 1)
                step(ts(first_slot[:, :], first_slot[:, :], -float(P), None, ALU.add))

            def embed_ids(t):
                dve.wait_ge(rec_psum, t + 1)
                step(nc.vector.tensor_copy(rec[:, :], bank[3][:, 0:4]))
                wait()
                step(stt(out=id_f[:, :], in0=rec[:, 0:1], scalar=256.0, in1=rec[:, 1:2], op0=ALU.mult, op1=ALU.add))
                wait()
                nc.vector.tensor_copy(id_i[:, :], id_f[:, :]).then_inc(id_ready, 1)
                ts(trained[:, 0:NTRAIN], train[:, :], id_f[:, 0:1], None, ALU.is_equal).then_inc(trained_ready, 1)

            def embed_sequences():
                step(ts(seq_is[:, :], col[:, 1:B + 1], rec[:, 3:4], None, ALU.is_equal))
                step(nc.vector.tensor_copy(valid_now[:, :], valid_next[:, :]))
                wait()
                step(ts(k_pad[:, :, :, DH:32].rearrange("p f i d -> p (f i) d"),
                        seq_is[:, :].unsqueeze(1).broadcast_to([P, G, B]), -1.0, None, ALU.add))
                step(ts(q_pad[:, :, :, :, DH:32].rearrange("p f r i d -> p (f r i) d"),
                        seq_is[:, :].unsqueeze(1).broadcast_to([P, H, B]), MASK, None, ALU.mult))
                step(ts(valid_next[:, :], rec[:, 2:3], 0.0, None, ALU.is_gt))

            def moments(src):
                step(nc.vector.bn_stats(stats[:, :], src))
                wait()
                step(nc.vector.bn_aggr(mv[:, :], stats[:, :]))
                wait()
                ts(var_eps[:, :], mv[:, 1:2], EPS, None, ALU.add).then_inc(var_ready, 1)

            def normalise(dst, src, k, ready):
                dve.wait_ge(rstd_ready, k)
                ts(dst, src, mv[:, 0:1], rstd[:, 0:1], ALU.subtract, ALU.mult).then_inc(ready, 1)

            def embed_rows(t):
                dve.wait_ge(row_gathered, t * 16 + 16)
                dve.wait_ge(delta_psum, t + 1)
                step(tt(h_next, w_row[:, :], bank[3][:, :], ALU.add))
                wait()
                moments(h_next)

            def transposed_keys(t):
                dve.wait_ge(qkT_psum, t + 1)
                for f in range(HALVES):
                    for i in range(4):
                        last = nc.vector.tensor_copy(kT[i * 32:i * 32 + 32, f, i, :],
                                                     bank[2][i * 32:i * 32 + 32, f * P:(f + 1) * P])
                    last.then_inc(kT_ready, 1)

            def route_top(k):
                dve.wait_ge(lexp_ready, k + 1)
                step(nc.vector.reciprocal(lrec[:, :], lsum[:, :]))
                wait()
                step(ts(score[:, :], lexp[:, :], lrec[:, 0:1], None, ALU.mult))
                wait()
                step(nc.vector.max(top[:, :], score[:, :]))
                wait()
                step(nc.vector.max_index(top_i[:, :], top[:, :], score[:, :]))
                step(red(topsum[:, :], top[:, :], X, ALU.add))
                wait()
                step(nc.vector.reciprocal(toprec[:, :], topsum[:, :]))
                step(nc.vector.tensor_copy(top_f[:, :], top_i[:, :]))
                wait()

            def route_mask(k):
                step(tt(is_e[:, :, :], col[:, 0:E].unsqueeze(1).broadcast_to([P, TOPK, E]),
                        top_f[:, :].unsqueeze(2).broadcast_to([P, TOPK, E]), ALU.is_equal))
                wait()
                step(red(mask[:, :], is_e[:, :, :].rearrange("p k e -> p e k"), X, ALU.add))
                wait()
                ts(mask_b[:, :], mask[:, :], valid[:, 0:1], None, ALU.mult).then_inc(mask_ready, 1)

            def route_ranks(k):
                dve.wait_ge(rank_psum, k + 1)
                step(tt(rank[:, :], taken[:, :], bank[7][:, 0:E], ALU.add))
                wait()
                step(tt(taken[:, :], taken[:, :], bank[7][:, E:2 * E], ALU.add))

            def route_lists(k):
                step(tt(picked[:, :, :], is_e[:, :, :], rank[:, :].unsqueeze(1).broadcast_to([P, TOPK, E]), ALU.mult))
                step(ts(far[:, :], valid[:, :], -FAR, FAR, ALU.mult, ALU.add))
                wait()
                step(red(rank_k[:, :], picked[:, :, :], X, ALU.add))
                wait()
                step(stt(out=dest_f[:, :], in0=rank_k[:, :], scalar=float(E), in1=top_f[:, :], op0=ALU.mult, op1=ALU.add))
                wait()
                dve.wait_ge(lists_free, k + 1)
                step(ts(dest[:, :], dest_f[:, :], far[:, 0:1], None, ALU.add))
                step(nc.vector.tensor_copy(list_rec[:, :, 0], my_slot[:, :].broadcast_to([P, TOPK])))
                step(ts(list_rec[:, :, 1].bitcast(F32), top[:, :], toprec[:, 0:1], None, ALU.mult))
                step(nc.vector.tensor_copy(valid[:, :], valid_now[:, :]))
                wait()
                ts(my_slot[:, :], my_slot[:, :], float(P), None, ALU.add).then_inc(list_ready, 1)

            pick_tokens(0)
            embed_ids(0)
            embed_sequences()
            pick_tokens(1)
            embed_rows(0)
            normalise(xn1, h_next, 1, xn1_ready)
            transposed_keys(0)
            dve.wait_ge(kv_ready, 1)
            embed_ids(1)
            steps.restart()
            with dve.Fori(0, ntiles) as n:
                def row_max(g):
                    dve.wait_ge(scores_psum, n * G + g + 1)
                    step(red(negmax[:, g, :], bank[g % 3][:, :].rearrange("p (i k) -> p i k", i=4), X, ALU.max))
                    wait()
                    ts(negmax[:, g, :], negmax[:, g, :], -1.0, None, ALU.mult).then_inc(max_ready, 1)

                for g in range(3):
                    row_max(g)
                embed_sequences()
                for g in range(G):
                    if g in BY_DVE:
                        dve.wait_ge(probsT_psum, n * G + g + 1)
                        nc.vector.tensor_copy(probsT[:, g % 2, :, :].rearrange("p r t -> p (r t)"),
                                              bank[4 + g % 2][:, :]).then_inc(probsT_dve, 1)
                    if g + 3 < G:
                        row_max(g + 3)
                    if g == 0:
                        route_top(n)
                    if g == 1:
                        route_mask(n)
                    if g == 3:
                        route_ranks(n)
                    if g == 4:
                        dve.wait_ge(h_ready, n + 1)
                        embed_rows(n + 1)
                    if g == 5:
                        normalise(xn1, h_next, n * 2 + 2, xn1_ready)
                        route_lists(n)
                dve.wait_ge(attn_psum, n + 1)
                for f in range(HALVES):
                    o = bank[6 + f][:, 0:16 * 17].rearrange("p (h d) -> p h d", d=17)
                    step(nc.vector.reciprocal(rden[:, f * 16:f * 16 + 16], o[:, :, DH]))
                wait()
                for f in range(HALVES):
                    o = bank[6 + f][:, 0:16 * 17].rearrange("p (h d) -> p h d", d=17)
                    last = tt(attn[:, f * 16:f * 16 + 16, :], o[:, :, 0:DH],
                              rden[:, f * 16:f * 16 + 16].unsqueeze(2).broadcast_to([P, 16, DH]), ALU.mult)
                last.then_inc(attn_ready, 1)
                pick_tokens(n + 2)
                dve.wait_ge(proj_psum, n + 1)
                dve.wait_ge(h2_stored, n * 16 + 16)
                tt(h2[:, :], h[:, :], bank[5][:, :], ALU.add).then_inc(h2_ready, 1)
                dve.wait_ge(h2_ready, n + 1)
                moments(h2[:, :])
                dve.wait_ge(rows_stored, n * 16 + 16)
                normalise(xn[:, :], h2[:, :], n * 2 + 3, xn2_ready)
                transposed_keys(n + 1)
                dve.wait_ge(kv_ready, n + 2)
                embed_ids(n + 2)
                dve.wait_ge(logits_psum, n + 1)
                step(red(lmax[:, :], bank[5][:, 0:E], X, ALU.max))
                wait()
                ts(lmax[:, :], lmax[:, :], -1.0, None, ALU.mult).then_inc(lmax_ready, 1)
                steps.restart()

            route_top(ntiles)
            route_mask(ntiles)
            route_ranks(ntiles)
            route_lists(ntiles)
            wait()
            dve.wait_ge(counts_psum, 1)
            step(nc.vector.tensor_copy(count_e[:, :], bank[0][0:E, 0:1]))
            wait()
            step(ts(more[:, :], tile_starts[0:E, :], count_e[:, 0:1], None, ALU.is_lt))
            wait()
            step(red(tiles_e[:, :], more[:, :], X, ALU.add))
            wait()
            ts(tiles_eb[:, :], tiles_e[:, :], 1.0, None, ALU.max).then_inc(tiles_ready, 1)
            dve.wait_ge(upto_psum, 1)
            step(nc.vector.tensor_copy(upto_e[:, :], bank[1][0:E, 0:1]))
            wait()
            ts(past[:, :], col[0:E, 0:TILES], upto_e[:, 0:1], None, ALU.is_ge).then_inc(past_ready, 1)
            dve.wait_ge(table_psum, 1)
            step(nc.vector.tensor_copy(t_exp[:, :], bank[2][0:1, 0:TILES]))
            step(nc.vector.tensor_copy(t_used[:, :], bank[3][0:1, 0:TILES]))
            step(ts(total_i[:, :], bank[4][0:1, 0:1], 1.0, None, ALU.add))
            step(nc.vector.tensor_copy(tab_upto[:, :], bank[5][0:1, 0:E]))
            wait()
            step(ts(t_end[:, :], t_exp[:, :], float(E), None, ALU.is_ge))
            step(tt(t_col[:, :], col[0:1, 0:TILES], t_used[:, :], ALU.subtract))
            step(ts(tab_pairs[:, :], total_i[:, :], 1, None, ALU.logical_shift_right))
            wait()
            step(stt(out=t_col[:, :], in0=t_col[:, :], scalar=float(E), in1=t_exp[:, :], op0=ALU.mult, op1=ALU.add))
            step(ts(t_exp[:, :], t_exp[:, :], float(E - 1), None, ALU.min))
            wait()
            step(ts(t_used[:, :], t_end[:, :], -1.0, 1.0, ALU.mult, ALU.add))
            step(nc.vector.tensor_copy(t_slot[:, :], t_exp[:, :]))
            step(ts(tab_exp[:, :], t_exp[:, :], 1.0, None, ALU.add))
            wait()
            step(tt(t_col[:, :], t_col[:, :], t_used[:, :], ALU.mult))
            step(ts(tab_slot[:, :], t_slot[:, :], SLOTS - 1, None, ALU.bitwise_and))
            wait()
            stt(out=tab_col[:, :], in0=t_end[:, :], scalar=float((NCH - 1) * E), in1=t_col[:, :], op0=ALU.mult,
                op1=ALU.add).then_inc(table_ready, 1)
            dve.wait_ge(reps_psum, 1)
            nc.vector.tensor_copy(rep_slot[:, :], bank[6][:, 0:B]).then_inc(reps_ready, 1)
            dve.wait_ge(table_ready, 1)
            dve.wait_ge(in_turn, 16)
            pairs = dve.value_load(tab_pairs[0:1, 0:1], min_val=1, max_val=PAIRS)

            def gate(g, u):
                c = dve.value_load(tab_col[0:1, bass.ds(g, 1)], min_val=0, max_val=NCH * E - 1)
                dve.wait_ge(silu_ready, g + 1)
                stt(out=hid[u][:, :, :].rearrange("p a c -> p (a c)"), in0=bank[2 + u][:, I:2 * I],
                    scalar=lists[:, bass.ds(c, 1), 1].bitcast(F32), in1=silu[:, :], op0=ALU.mult,
                    op1=ALU.mult).then_inc(hid_ready, 1)

            gate(0, 0)
            steps.restart()
            with dve.Fori(0, pairs) as m:
                for u in range(2):
                    g = m * 2 + u
                    dve.wait_ge(hidT_psum, g + 1)
                    nc.vector.tensor_copy(hidT[u][:, :, :].rearrange("p c t -> p (c t)"),
                                          bank[4 + u][0:IP, 0:IC * P]).then_inc(hidT_ready, 1)
                    gate(g + 1, 1 - u)
                    dve.wait_ge(y_free, g + 1)
                    dve.wait_ge(y_psum, g + 1)
                    nc.vector.tensor_copy(y[u], bank[6 + u][:, :]).then_inc(y_ready, 1)
                steps.restart()

        @block.tensor
        def _(pe):
            mm, tr = nc.tensor.matmul, nc.tensor.transpose
            pe.wait_ge(consts, 1)
            groups = [[(delta_nat[:, c, :], NTRAIN, c * P) for c in range(C)]]
            groups += [[(wq_nat[:, r, c * P:(c + 1) * P], P, r * P) for r in range(C)] for c in range(C)]
            groups += [[(wkv_nat[:, s, c * P:(c + 1) * P], P, (c % 2) * 2 * P + s * P) for c in (2 * i, 2 * i + 1)
                        for s in range(2)] for i in range(2)]
            groups += [[(wo_nat[:, r, c * P:(c + 1) * P], P, r * P) for r in range(C)] for c in range(C)]
            groups += [[(gw_nat[:, c * P:(c + 1) * P], P, c * E) for c in range(C)]]
            pe.wait_ge(weights_in, 96)
            for i, pieces in enumerate(groups):
                if i >= 4:
                    pe.wait_ge(prep_out, i - 3)
                for src, rows, at in pieces:
                    k = src.shape[0]
                    last = tr(bank[i % 4][0:rows, at:at + k], src, ident[0:k, 0:k])
                last.then_inc(prep_psum, 1)
            pe.wait_ge(first_ready, 1)
            mm(bank[7][:, 0:B], earlier[:, :], first[:, :], start=True, stop=True)
            mm(bank[7][:, 64:64 + B], ones[:, :], first[:, :], start=True, stop=True).then_inc(ranks_psum, 1)

            pe.wait_ge(ntiles_ready, 1)
            ntiles = pe.value_load(ntiles_i[0:1, 0:1], min_val=1, max_val=B)
            pe.wait_ge(prep_out, PREP)

            def embed_records(t):
                pe.wait_ge(pick_ready, t + 1)
                for b in range(B):
                    last = mm(bank[3][:, 0:4], pick[:, b, :], attrs[:, b, :], start=(b == 0), stop=(b == B - 1))
                last.then_inc(rec_psum, 1)

            def embed_trained(t):
                pe.wait_ge(trained_ready, t + 1)
                tr(bank[3][:, 128:256], trained[:, :], ident[:, :]).then_inc(trainedT_psum, 1)

            def embed_delta(t):
                pe.wait_ge(trainedT_ready, t + 1)
                mm(bank[3][:, :], trainedT[:, :], delta[:, :], start=True, stop=True).then_inc(delta_psum, 1)

            def transpose_rows(src, dst):
                for c in range(C):
                    last = tr(dst[:, c * P:(c + 1) * P], src[:, c * P:(c + 1) * P], ident[:, :])
                return last

            def embed_transposed(t):
                pe.wait_ge(xn1_ready, t + 1)
                transpose_rows(xn1, bank[3]).then_inc(xn1T_psum, 1)

            def queries(t, chunks):
                if chunks[0] == 0:
                    pe.wait_ge(xn1T_ready, t + 1)
                for c in chunks:
                    last = mm(bank[2][:, :], xn1T[:, c, :], wqT[:, c, :], start=(c == 0), stop=(c == C - 1))
                if c == C - 1:
                    last.then_inc(q_psum, 1)

            def keys_values(t):
                for c in range(C):
                    last = mm(bank[0][:, 0:2 * KVD], xn1T[:, c, :], wkvT[:, c, :], start=(c == 0), stop=(c == C - 1))
                last.then_inc(kv_psum, 1)

            def transpose_queries(t):
                pe.wait_ge(q_ready, t + 1)
                pe.wait_ge(kv_ready, t + 1)
                for f in range(HALVES):
                    for r in range(R):
                        tr(bank[f][:, r * P:(r + 1) * P], q_pad[:, f, r, :, :].rearrange("p i d -> p (i d)"), ident[:, :])
                    last = tr(bank[2][:, f * P:(f + 1) * P], k_pad[:, f, :, :].rearrange("p i d -> p (i d)"), ident[:, :])
                last.then_inc(qkT_psum, 1)

            def list_ranks(k):
                pe.wait_ge(mask_ready, k + 1)
                mm(bank[7][:, 0:E], earlier_b[:, :], mask_b[:, :], start=True, stop=True)
                mm(bank[7][:, E:2 * E], ones_b[:, :], mask_b[:, :], start=True, stop=True).then_inc(rank_psum, 1)

            embed_records(0)
            embed_trained(0)
            embed_delta(0)
            embed_transposed(0)
            queries(0, range(C))
            keys_values(0)
            transpose_queries(0)
            embed_records(1)
            with pe.Fori(0, ntiles) as n:
                pe.wait_ge(qT_ready, n * 2 + 2)
                pe.wait_ge(kT_ready, n * 2 + 2)

                def scores(g):
                    f, r = g // R, g % R
                    mm(bank[g % 3][:, :], qT[:, f, r, :], kT[:, f, :, :].rearrange("p i t -> p (i t)"),
                       start=True, stop=True).then_inc(scores_psum, 1)

                def transpose_probs(g):
                    pe.wait_ge(probs_ready, n * G + g + 1)
                    for i in range(4):
                        last = tr(bank[4 + g % 2][:, i * P:(i + 1) * P], probs[:, g % 2, i, :], ident[:, :])
                    last.then_inc(probsT_psum, 1)

                for g in range(3):
                    scores(g)
                embed_trained(n + 1)
                transpose_probs(0)
                for g in range(G):
                    if g + 3 < G:
                        scores(g + 3)
                    if g == 0:
                        embed_delta(n + 1)
                    if g + 1 < G:
                        transpose_probs(g + 1)
                    if g == 2:
                        list_ranks(n)
                    if g in BY_DVE:
                        pe.wait_ge(probsT_dve, n * len(BY_DVE) + BY_DVE.index(g) + 1)
                    else:
                        pe.wait_ge(probsT_act, n * len(BY_ACT) + BY_ACT.index(g) + 1)
                    f, r = g // R, g % R
                    for i in range(4):
                        hd = i * R + r
                        last = mm(bank[6 + f][:, hd * 17:hd * 17 + 17], probsT[:, g % 2, i, :], v_aug[:, f * 4 + i, :],
                                  start=True, stop=True)
                    if g == 6:
                        embed_transposed(n + 1)
                last.then_inc(attn_psum, 1)
                queries(n + 1, (0, 1))
                pe.wait_ge(attn_ready, n + 1)
                transpose_rows(attn[:, :, :].rearrange("p h d -> p (h d)"), bank[4]).then_inc(attnT_psum, 1)
                queries(n + 1, (2,))
                pe.wait_ge(attnT_ready, n + 1)
                for c in range(C):
                    last = mm(bank[5][:, :], xnT[:, c, :], woT[:, c, :], start=(c == 0), stop=(c == C - 1))
                last.then_inc(proj_psum, 1)
                queries(n + 1, (3,))
                keys_values(n + 1)
                pe.wait_ge(xn2_ready, n + 1)
                transpose_rows(xn, bank[4]).then_inc(xn2T_psum, 1)
                transpose_queries(n + 1)
                embed_records(n + 2)
                pe.wait_ge(xn2T_ready, n + 1)
                for c in range(C):
                    last = mm(bank[5][:, 0:E], xnT[:, c, :], gwT[:, c, :], start=(c == 0), stop=(c == C - 1))
                last.then_inc(logits_psum, 1)

            list_ranks(ntiles)
            hold(pe, list_ready, ntiles + 1, held)
            hold(pe, qT_ready, ntiles * 2 + 2, held)
            tr(bank[0][0:E, 0:P], taken[:, :], ident[:, :]).then_inc(counts_psum, 1)
            pe.wait_ge(tiles_ready, 1)
            mm(bank[1][0:E, 0:1], upto[0:E, 0:E], tiles_eb[:, :], start=True, stop=True).then_inc(upto_psum, 1)
            pe.wait_ge(past_ready, 1)
            mm(bank[2][0:1, 0:TILES], ones_b[0:E, 0:1], past[:, :], start=True, stop=True)
            mm(bank[3][0:1, 0:TILES], tiles_eb[:, :], past[:, :], start=True, stop=True)
            mm(bank[4][0:1, 0:1], ones_b[0:E, 0:1], tiles_eb[:, :], start=True, stop=True)
            mm(bank[5][0:1, 0:E], tiles_eb[:, :], upto[0:E, 0:E], start=True, stop=True).then_inc(table_psum, 1)
            pe.wait_ge(chosen_ready, 1)
            for b in range(B):
                last = mm(bank[6][:, b:b + 1], same[:, b * S:(b + 1) * S], chosen[:, b:b + 1], start=True, stop=True)
            last.then_inc(reps_psum, 1)

            pe.wait_ge(table_ready, 1)
            pairs = pe.value_load(tab_pairs[0:1, 0:1], min_val=1, max_val=PAIRS)

            def transpose_gathered(g, u, turn):
                pe.wait_ge(xg_in[u], turn * 16)
                for c in range(C):
                    last = tr(bank[u][:, c * P:(c + 1) * P], xg[u][:, :, c], ident[:, :])
                last.then_inc(xgT_psum, 1)

            def slot_of_tile(g):
                return pe.value_load(tab_slot[0:1, bass.ds(g, 1)], min_val=0, max_val=SLOTS - 1)

            def expert_of_tile(g):
                return pe.value_load(tab_exp[0:1, bass.ds(g, 1)], min_val=1, max_val=E)

            def gate_up(g, u, slot, need):
                pe.wait_ge(expert_in, need)
                pe.wait_ge(xgT_ready, g + 1)
                for c in range(C):
                    last = mm(bank[2 + u][:, 0:2 * I], xgT[u][:, c, :],
                              wgu[:, bass.ds(slot, 1), :, c * I:(c + 1) * I].rearrange("p o w i -> p (o w) i"),
                              start=(c == 0), stop=(c == C - 1))
                last.then_inc(gu_psum, 1)

            transpose_gathered(0, 0, 1)
            transpose_gathered(1, 1, 1)
            gate_up(0, 0, slot_of_tile(0), expert_of_tile(0))
            with pe.Fori(0, pairs) as m:
                for u in range(2):
                    g = m * 2 + u
                    slot = slot_of_tile(g) if u == 0 else slot_next
                    slot_next, expert_next = slot_of_tile(g + 1), expert_of_tile(g + 1)
                    pe.wait_ge(hid_ready, g + 1)
                    for c in range(IC):
                        last = tr(bank[4 + u][0:IP, c * P:(c + 1) * P], hid[u][:, :, c], ident[:, :])
                    last.then_inc(hidT_psum, 1)
                    gate_up(g + 1, 1 - u, slot_next, expert_next)
                    transpose_gathered(g + 2, u, m + 2)
                    pe.wait_ge(hidT_ready, g + 1)
                    pe.wait_ge(y_ready, g + 1)
                    for c in range(IC):
                        last = mm(bank[6 + u][:, :], hidT[u][:, c, :],
                                  wdn[:, bass.ds(slot, 1), c * D:(c + 1) * D].rearrange("p o n -> p (o n)"),
                                  start=(c == 0), stop=(c == IC - 1))
                    last.then_inc(y_psum, 1)


_INS = ['x', 'L0_tok_W', 'L0_tok_delta_values', 'L0_tok_token_indices', 'L0_attn_w_q', 'L0_attn_w_k', 'L0_attn_w_v',
        'L0_attn_w_o', 'L0_ffn_gate_weight', 'L0_ffn_w_gate', 'L0_ffn_w_up', 'L0_ffn_w_down']
_OUTS = [((16, 128, 512), 'float32')]
build = dedup_moe_lm_tower


def kernel(**inputs):
    import numpy as _np
    import concourse.bacc as _bacc
    from concourse import mybir as _mybir
    from concourse.bass_utils import run_bass_kernel_spmd as _run

    nc = _bacc.Bacc("TRN2", target_bir_lowering=False, num_devices=1)
    arrays, args = {}, []
    for name in _INS:
        a = _np.ascontiguousarray(inputs[name])
        arrays[f"in_{name}_dram"] = a
        args.append(nc.dram_tensor(f"in_{name}_dram", a.shape, _mybir.dt.from_np(a.dtype), kind="ExternalInput").ap())
    for i, (shape, dtype) in enumerate(_OUTS):
        dt = _mybir.dt.from_np(_np.dtype(dtype))
        args.append(nc.dram_tensor(f"out_{i}_dram", shape, dt, kind="ExternalOutput").ap())
    dedup_moe_lm_tower(nc, *args)
    r = _run(nc, [arrays], core_ids=[0])
    return r.results[0]["out_0_dram"]
```

```python
from contextlib import ExitStack

import concourse.bass as bass
from concourse import mybir

P = 128
F32 = mybir.dt.float32
BF16 = mybir.dt.bfloat16
I32 = mybir.dt.int32
U32 = mybir.dt.uint32
ALU = mybir.AluOpType
ACT = mybir.ActivationFunctionType
X = mybir.AxisListType.X

EPS = 1e-5
MASK = float(2.0 ** 100)
FAR = float(2 ** 22)
SLOTS = 4


class Chain:

    def __init__(self, eng, sem):
        self.eng, self.sem, self.count = eng, sem, 0

    def mark(self, ins):
        ins.then_inc(self.sem, 1)
        self.count += 1

    def wait(self):
        self.eng.wait_ge(self.sem, self.count)

    def restart(self):
        self.wait()
        self.eng.sem_clear(self.sem)
        self.count = 0


def hold(eng, sem, value, held):
    eng.wait_ge(sem, value)
    eng.sem_inc(held, 1)


def dedup_moe_lm_tower(nc, x, tok_w, tok_delta, tok_idx, w_q, w_k, w_v, w_o, gate_w, w_gate, w_up, w_down, out):
    B, S = x.shape
    VOCAB, D = tok_w.shape
    NTRAIN = tok_idx.shape[0]
    KVD = w_k.shape[0]
    E, _, I = w_gate.shape
    TOPK = 8
    DH = 16
    H = D // DH
    G = KVD // DH
    R = H // G
    C = D // P
    IC, IP = 2, I // 2
    ROWS = B * S
    NCH = ROWS // P + 1
    HALVES = G // 4
    PAIRS = (ROWS * TOPK // P + E) // 2
    TILES = 2 * PAIRS + 8
    assert S == P and C == 4 and R == 4 and G == 8 and H * DH == D

    xn_dram = nc.dram_tensor("xn_rows", (ROWS + P, D), F32).ap()
    y_dram = nc.dram_tensor("y_rows", (ROWS + P, D), F32).ap()
    list_dram = nc.dram_tensor("expert_lists", (NCH * P * E, 2), I32).ap()
    list_rows = list_dram.rearrange("(c r e) t -> r c (e t)", r=P, e=E)

    with ExitStack() as ctx:
        def sb(name, shape, dt=F32):
            return ctx.enter_context(nc.sbuf_tensor(name, shape, dt))

        def sem(name):
            return ctx.enter_context(nc.semaphore(name))

        bank = [ctx.enter_context(nc.psum_tensor(f"bank{i}", [P, 512], F32)) for i in range(8)]

        ident = sb("ident", [P, P])
        earlier = sb("earlier", [P, P])
        earlier_b = sb("earlier_b", [P, P], BF16)
        upto = sb("upto", [P, P], BF16)
        ones = sb("ones", [P, P])
        ones_b = sb("ones_b", [P, P], BF16)
        col = sb("col", [P, 256])
        row = sb("row", [P, 1])
        tile_starts = sb("tile_starts", [P, 16])
        zeros = sb("zeros", [P, D])
        pad_list = sb("pad_list", [P, E, 2], I32)

        wq_nat = sb("wq_nat", [P, C, D])
        wo_nat = sb("wo_nat", [P, C, D])
        wkv_nat = sb("wkv_nat", [P, 2, D])
        gw_nat = sb("gw_nat", [E, D])
        delta_nat = sb("delta_nat", [P, C, NTRAIN])
        wqT = sb("wqT", [P, C, D])
        woT = sb("woT", [P, C, D])
        wkvT = sb("wkvT", [P, C, 2 * KVD])
        gwT = sb("gwT", [P, C, E])
        delta = sb("delta", [NTRAIN, D])

        ids_row_i = sb("ids_row_i", [P, ROWS], I32)
        ids_col_i = sb("ids_col_i", [P, B], I32)
        train_i = sb("train_i", [P, NTRAIN], I32)
        ids_col = sb("ids_col", [P, B])
        train = sb("train", [P, NTRAIN])
        scratch = sb("scratch", [P, ROWS])
        same = sb("same", [P, ROWS], BF16)
        same_before = sb("same_before", [P, ROWS], BF16)
        first = sb("first", [P, B])
        rank_in_seq = sb("rank_in_seq", [P, B])
        distinct = sb("distinct", [P, B])
        keep = sb("keep", [P, B])
        fill = sb("fill", [P, B + 1])
        skips = sb("skips", [P, B])
        offset = sb("offset", [P, B])
        slot_of = sb("slot_of", [P, B])
        first_slot = sb("first_slot", [P, B])
        chosen = sb("chosen", [P, B], I32)
        chosen_low = sb("chosen_low", [P, B], I32)
        place = sb("place", [P, B])
        tab_tile = sb("tab_tile", [1, B], I32)
        onehot = scratch
        attrs = sb("attrs", [P, B, 4], BF16)
        low = sb("low", [P, B], I32)
        high = sb("high", [P, B], I32)
        ntiles_i = sb("ntiles_i", [1, 1], I32)

        pick = sb("pick", [P, B, P], BF16)
        rec = sb("rec", [P, 4])
        id_f = sb("id_f", [P, 1])
        id_i = sb("id_i", [P, 1], I32)
        seq_is = sb("seq_is", [P, B])
        valid_next = sb("valid_next", [P, 1])
        valid_now = sb("valid_now", [P, 1])
        valid = sb("valid", [P, 1])
        trained = sb("trained", [P, P])
        trainedT = sb("trainedT", [NTRAIN, P])
        w_row = sb("w_row", [P, D])
        h = sb("h", [P, D])
        h_next = scratch[:, 0:D]
        xn1 = scratch[:, D:2 * D]
        xn1T = scratch[:, 2 * D:3 * D].rearrange("p (c t) -> p c t", c=C)
        stats = sb("stats", [P, 2, 6])
        mv = sb("mv", [P, 2])
        minus_half = sb("minus_half", [P, 1])
        var_eps = sb("var_eps", [P, 1])
        rstd = sb("rstd", [P, 1])
        xn = sb("xn", [P, D])
        xnT = sb("xnT", [P, C, P])
        q_pad = sb("q_pad", [P, HALVES, R, 4, 32])
        k_pad = sb("k_pad", [P, HALVES, 4, 32])
        v_aug = sb("v_aug", [P, G, DH + 1])
        qT = sb("qT", [P, HALVES, R, P])
        kT = ids_row_i[:, 0:HALVES * 4 * P].bitcast(F32).rearrange("p (f i t) -> p f i t", f=HALVES, i=4)
        negmax = sb("negmax", [P, G, 4])
        probs = wq_nat[:, 0:2, :].rearrange("p u (i t) -> p u i t", i=4)
        probsT = wq_nat[:, 2:4, :].rearrange("p u (i t) -> p u i t", i=4)
        rden = sb("rden", [P, H])
        attn = sb("attn", [P, H, DH])
        h2 = sb("h2", [P, D])
        lmax = sb("lmax", [P, 1])
        lexp = sb("lexp", [P, E])
        lsum = sb("lsum", [P, 1])
        lrec = sb("lrec", [P, 1])
        score = sb("score", [P, E])
        top = sb("top", [P, TOPK])
        top_i = sb("top_i", [P, TOPK], U32)
        top_f = sb("top_f", [P, TOPK])
        topsum = sb("topsum", [P, 1])
        toprec = sb("toprec", [P, 1])
        is_e = sb("is_e", [P, TOPK, E])
        picked = sb("picked", [P, TOPK, E])
        mask = sb("mask", [P, E])
        mask_b = sb("mask_b", [P, E], BF16)
        rank = sb("rank", [P, E])
        taken = sb("taken", [P, E])
        rank_k = sb("rank_k", [P, TOPK])
        far = sb("far", [P, 1])
        dest_f = sb("dest_f", [P, TOPK])
        dest = sb("dest", [P, TOPK], I32)
        list_rec = sb("list_rec", [P, TOPK, 2], I32)
        my_slot = sb("my_slot", [P, 1])

        lists = sb("lists", [P, NCH * E, 2], I32)
        count_e = sb("count_e", [E, 1])
        more = sb("more", [E, 16])
        tiles_e = sb("tiles_e", [E, 1])
        tiles_eb = sb("tiles_eb", [E, 1], BF16)
        upto_e = sb("upto_e", [E, 1])
        past = sb("past", [E, TILES], BF16)
        t_exp = sb("t_exp", [1, TILES])
        t_used = sb("t_used", [1, TILES])
        t_end = sb("t_end", [1, TILES])
        t_col = sb("t_col", [1, TILES])
        t_slot = sb("t_slot", [1, TILES], I32)
        total_i = sb("total_i", [1, 1], I32)
        tab_col = sb("tab_col", [1, TILES], I32)
        tab_exp = sb("tab_exp", [1, TILES], I32)
        tab_slot = sb("tab_slot", [1, TILES], I32)
        tab_upto = sb("tab_upto", [1, E], I32)
        tab_pairs = sb("tab_pairs", [1, 1], I32)

        room = sb("room", [P, max(B * D, SLOTS * 2 * C * I)])
        wgu = room[:, 0:SLOTS * 2 * C * I].rearrange("p (s w n) -> p s w n", s=SLOTS, w=2)
        y_tiles = room[:, 0:B * D].rearrange("p (n d) -> p n d", n=B)
        wdn = sb("wdn", [IP, SLOTS, IC * D])
        gidx = [sb(f"gidx{u}", [P, 1], I32) for u in range(2)]
        sidx = [sb(f"sidx{u}", [P, 1], I32) for u in range(2)]
        xg = [wo_nat[:, u, :].rearrange("p (a c) -> p a c", c=C) for u in range(2)]
        xgT = [wo_nat[:, 2 + u, :].rearrange("p (c t) -> p c t", c=C) for u in range(2)]
        y = [wkv_nat[:, u, :] for u in range(2)]
        final = [wq_nat[:, u, :] for u in range(4)]
        silu = sb("silu", [P, I])
        hid = [sb(f"hid{u}", [P, IP, IC]) for u in range(2)]
        hidT = [sb(f"hidT{u}", [IP, IC, P]) for u in range(2)]

        consts = sem("consts")
        ids_in = sem("ids_in")
        weights_in = sem("weights_in")
        pads_written = sem("pads_written")
        prep_psum = sem("prep_psum")
        prep_out = sem("prep_out")
        same_ready = sem("same_ready")
        before_ready = sem("before_ready")
        seen_psum = sem("seen_psum")
        first_ready = sem("first_ready")
        ranks_psum = sem("ranks_psum")
        places_ready = sem("places_ready")
        onehot_psum = sem("onehot_psum")
        onehot_ready = sem("onehot_ready")
        y_in = sem("y_in")
        final_psum = sem("final_psum")
        final_even = sem("final_even")
        final_odd = sem("final_odd")
        ntiles_ready = sem("ntiles_ready")
        held = sem("held")
        dve_steps = sem("dve_steps")
        act_steps = sem("act_steps")
        pool_steps = sem("pool_steps")
        pick_ready = sem("pick_ready")
        rec_psum = sem("rec_psum")
        id_ready = sem("id_ready")
        row_gathered = sem("row_gathered")
        trained_ready = sem("trained_ready")
        trainedT_psum = sem("trainedT_psum")
        trainedT_ready = sem("trainedT_ready")
        delta_psum = sem("delta_psum")
        var_ready = sem("var_ready")
        rstd_ready = sem("rstd_ready")
        xn1_ready = sem("xn1_ready")
        xn1T_psum = sem("xn1T_psum")
        xn1T_ready = sem("xn1T_ready")
        q_psum = sem("q_psum")
        kv_psum = sem("kv_psum")
        q_ready = sem("q_ready")
        kv_ready = sem("kv_ready")
        h_ready = sem("h_ready")
        qkT_psum = sem("qkT_psum")
        qT_ready = sem("qT_ready")
        kT_ready = sem("kT_ready")
        scores_psum = sem("scores_psum")
        max_ready = sem("max_ready")
        probs_ready = sem("probs_ready")
        probsT_psum = sem("probsT_psum")
        probsT_dve = sem("probsT_dve")
        probsT_act = sem("probsT_act")
        attn_psum = sem("attn_psum")
        attn_ready = sem("attn_ready")
        attnT_psum = sem("attnT_psum")
        attnT_ready = sem("attnT_ready")
        proj_psum = sem("proj_psum")
        xn2_ready = sem("xn2_ready")
        xn2T_psum = sem("xn2T_psum")
        xn2T_ready = sem("xn2T_ready")
        logits_psum = sem("logits_psum")
        lmax_ready = sem("lmax_ready")
        lexp_ready = sem("lexp_ready")
        mask_ready = sem("mask_ready")
        rank_psum = sem("rank_psum")
        list_ready = sem("list_ready")
        rows_stored = sem("rows_stored")
        h2_ready = sem("h2_ready")
        h2_stored = sem("h2_stored")
        lists_scattered = sem("lists_scattered")
        lists_free = sem("lists_free")
        other_lists_in = sem("other_lists_in")
        in_turn = sem("in_turn")
        y_free = sem("y_free")
        counts_psum = sem("counts_psum")
        tiles_ready = sem("tiles_ready")
        upto_psum = sem("upto_psum")
        past_ready = sem("past_ready")
        table_psum = sem("table_psum")
        table_ready = sem("table_ready")
        slot_in = [sem(f"slot_in{s}") for s in range(SLOTS)]
        expert_in = sem("expert_in")
        xg_in = [sem(f"xg_in{u}") for u in range(2)]
        xgT_psum = sem("xgT_psum")
        xgT_ready = sem("xgT_ready")
        gu_psum = sem("gu_psum")
        silu_ready = sem("silu_ready")
        hid_ready = sem("hid_ready")
        hidT_psum = sem("hidT_psum")
        hidT_ready = sem("hidT_ready")
        y_psum = sem("y_psum")
        y_ready = sem("y_ready")
        final_out = [sem(f"final_out{u}") for u in range(4)]

        gate_v = w_gate.rearrange("e (p c) i -> e p (c i)", c=C)
        up_v = w_up.rearrange("e (p c) i -> e p (c i)", c=C)
        down_v = w_down.rearrange("e (p c) n -> e p (c n)", c=IC)

        SCORE_BANKS = (0, 2, 1)
        BY_DVE = (0, 4)
        BY_ACT = tuple(g for g in range(G) if g not in BY_DVE)

        PREP = 12
        block = ctx.enter_context(nc.Block())

        @block.sync
        def _(sp):
            sp.sem_inc(rows_stored, 16)
            sp.sem_inc(h2_stored, 16)
            sp.dma_start(ids_col_i[:, :], x.rearrange("b s -> s b"), allow_slow_non_contiguous=True
                         ).then_inc(ids_in, 16)
            sp.dma_start(ids_row_i[:, :], x.rearrange("(o b) s -> o (b s)", o=1).broadcast_to([P, ROWS])
                         ).then_inc(ids_in, 16)
            sp.dma_start(train_i[:, :], tok_idx.rearrange("(o n) -> o n", o=1).broadcast_to([P, NTRAIN])
                         ).then_inc(ids_in, 16)
            sp.dma_start(delta_nat[:, :, :], tok_delta.rearrange("(c p n) -> p c n", c=C, p=P)).then_inc(weights_in, 16)
            sp.dma_start(wq_nat[:, :, :], w_q.rearrange("(c p) d -> p c d", p=P)).then_inc(weights_in, 16)
            sp.dma_start(wkv_nat[:, 0, :], w_k).then_inc(weights_in, 16)
            sp.dma_start(wkv_nat[:, 1, :], w_v).then_inc(weights_in, 16)
            sp.dma_start(wo_nat[:, :, :], w_o.rearrange("(c p) d -> p c d", p=P)).then_inc(weights_in, 16)
            sp.dma_start(gw_nat[:, :], gate_w).then_inc(weights_in, 16)
            def fill_rows(rows):
                sp.dma_start(rows.rearrange("(c p) d -> p c d", p=P), zeros[:, :].unsqueeze(1).broadcast_to([P, NCH, D])
                             ).then_inc(pads_written, 16)

            sp.wait_ge(consts, 1)
            sp.dma_start(list_rows, pad_list[:, :, :].rearrange("p e t -> p (e t)").unsqueeze(1)
                         .broadcast_to([P, NCH, 2 * E])).then_inc(pads_written, 16)
            fill_rows(y_dram)
            sp.wait_ge(row_gathered, 16)
            fill_rows(xn_dram)
            sp.wait_ge(row_gathered, 32)
            def load_expert(e, s):
                sp.dma_start(wgu[:, s, 0, :], gate_v[e]).then_inc(slot_in[s], 16)
                sp.dma_start(wgu[:, s, 1, :], up_v[e]).then_inc(slot_in[s], 16)
                sp.dma_start(wdn[:, s, :], down_v[e]).then_inc(slot_in[s], 16)

            for s in range(SLOTS):
                load_expert(s, s)
            sp.wait_ge(ntiles_ready, 1)
            ntiles = sp.value_load(ntiles_i[0:1, 0:1], min_val=1, max_val=B)
            sp.wait_ge(pads_written, 48)
            with sp.Fori(0, ntiles) as n:
                sp.wait_ge(h2_ready, n * 2 + 2)
                sp.dma_start(y_dram[bass.ts(n, P), :], h2[:, :]).then_inc(h2_stored, 16)
                sp.wait_ge(xn2_ready, n + 1)
                sp.dma_start(xn_dram[bass.ts(n, P), :], xn[:, :]).then_inc(rows_stored, 16)
            def landed(turn, s):
                sp.wait_ge(slot_in[s], turn * 48)
                sp.sem_inc(expert_in, 1)

            sp.wait_ge(table_ready, 1)
            for s in range(2):
                landed(1, s)
            sp.wait_ge(xg_in[1], 16)
            sp.dma_start(lists[:, 2 * E:, :].rearrange("p (c e) t -> p c (e t)", e=E), list_rows[:, 2:, :]
                         ).then_inc(other_lists_in, 16)
            with sp.Fori(0, E // SLOTS - 1) as r:
                for s in range(SLOTS):
                    landed(r + 1 + (s + 2) // SLOTS, (s + 2) % SLOTS)
                    done = sp.value_load(tab_upto[0:1, bass.ds(r * SLOTS + s, 1)], min_val=1, max_val=TILES)
                    sp.wait_ge(y_psum, done)
                    load_expert((r + 1) * SLOTS + s, s)
            for s in range(2, SLOTS):
                landed(E // SLOTS, s)
            pairs = sp.value_load(tab_pairs[0:1, 0:1], min_val=1, max_val=PAIRS)
            hold(sp, in_turn, pairs * 32 + 16, held)
            with sp.Fori(0, ntiles) as n:
                sp.dma_start(y_tiles[:, bass.ds(n, 1), :].rearrange("p o d -> p (o d)"), y_dram[bass.ts(n, P), :]
                             ).then_inc(y_in, 16)
            for b in range(B):
                sp.wait_ge(final_odd if b % 2 else final_even, b // 2 + 1)
                sp.dma_start(out[b], final[b % 4]).then_inc(final_out[b % 4], 16)
            for u in range(4):
                sp.wait_ge(final_out[u], 16 * (B // 4))

        @block.gpsimd
        def _(pool):
            steps = Chain(pool, pool_steps)
            pool.sem_inc(lists_free, 1)
            pool.sem_inc(y_free, 1)
            iota = nc.gpsimd.iota
            kw = dict(allow_small_or_imprecise_dtypes=True)
            steps.mark(nc.gpsimd.memset(ones[:, :], 1.0))
            steps.mark(nc.gpsimd.memset(ones_b[:, :], 1.0))
            steps.mark(nc.gpsimd.memset(zeros[:, :], 0.0))
            steps.mark(nc.gpsimd.memset(pad_list[:, :, :], 0))
            steps.mark(nc.gpsimd.memset(taken[:, :], 0.0))
            steps.mark(nc.gpsimd.memset(trained[:, :], 0.0))
            steps.mark(nc.gpsimd.memset(minus_half[:, :], -0.5))
            for t in (valid_next, valid):
                steps.mark(nc.gpsimd.memset(t[:, :], 0.0))
            for t in (lexp, lsum):
                steps.mark(nc.gpsimd.memset(t[:, :], 1.0))
            steps.mark(iota(col[:, :], [[1, 256]], base=0, channel_multiplier=0, **kw))
            steps.mark(iota(row[:, :], [[1, 1]], base=0, channel_multiplier=1, **kw))
            steps.mark(iota(my_slot[:, :], [[1, 1]], base=-P, channel_multiplier=1, **kw))
            steps.mark(iota(tile_starts[:, :], [[P, 16]], base=0, channel_multiplier=0, **kw))
            steps.wait()
            steps.mark(iota(pad_list[:, :, 0], [[0, E]], base=ROWS, channel_multiplier=1))
            steps.mark(nc.gpsimd.affine_select(out=ident[:, :], in_=ones[:, :], compare_op=ALU.is_equal, fill=0.0,
                                               base=0, pattern=[[-1, P]], channel_multiplier=1))
            steps.mark(nc.gpsimd.affine_select(out=earlier[:, :], in_=ones[:, :], compare_op=ALU.is_gt, fill=0.0,
                                               base=0, pattern=[[1, P]], channel_multiplier=-1))
            steps.mark(nc.gpsimd.affine_select(out=earlier_b[:, :], in_=ones_b[:, :], compare_op=ALU.is_gt, fill=0.0,
                                               base=0, pattern=[[1, P]], channel_multiplier=-1))
            steps.mark(nc.gpsimd.affine_select(out=upto[:, :], in_=ones_b[:, :], compare_op=ALU.is_ge, fill=0.0,
                                               base=0, pattern=[[1, P]], channel_multiplier=-1))
            steps.wait()
            nc.gpsimd.memset(q_pad[:, :, :, :, :], 0.0).then_inc(consts, 1)

            pool.wait_ge(ntiles_ready, 1)
            ntiles = pool.value_load(ntiles_i[0:1, 0:1], min_val=1, max_val=B)

            def gather_rows(t):
                hold(pool, id_ready, t + 1, held)
                nc.gpsimd.indirect_dma_start(w_row[:, :], None, tok_w,
                                             bass.IndirectOffsetOnAxis(ap=id_i[:, 0:1], axis=0),
                                             bounds_check=VOCAB - 1, oob_is_err=False).then_inc(row_gathered, 16)

            def inverse_root(k):
                pool.wait_ge(var_ready, k)
                nc.gpsimd.tensor_tensor(rstd[:, :], var_eps[:, :], minus_half[:, :], ALU.pow).then_inc(rstd_ready, 1)

            def scatter_lists(ks):
                for k in ks:
                    nc.gpsimd.indirect_dma_start(list_dram, bass.IndirectOffsetOnAxis(ap=dest[:, k:k + 1], axis=0),
                                                 list_rec[:, k, :], None, bounds_check=NCH * P * E - 1,
                                                 oob_is_err=False).then_inc(lists_scattered, 16)

            def lists_done(k):
                pool.wait_ge(lists_scattered, k * (16 * TOPK) + 16 * TOPK)
                pool.sem_inc(lists_free, 1)

            gather_rows(0)
            inverse_root(1)
            pool.wait_ge(pads_written, 48)
            with pool.Fori(0, ntiles) as n:
                gather_rows(n + 1)
                inverse_root(n * 2 + 2)
                hold(pool, list_ready, n + 1, held)
                scatter_lists(range(TOPK))
                inverse_root(n * 2 + 3)
                lists_done(n)
            hold(pool, list_ready, ntiles + 1, held)
            scatter_lists(range(TOPK))
            lists_done(ntiles)

            pool.dma_start(lists[:, 0:2 * E, :].rearrange("p (c e) t -> p c (e t)", e=E), list_rows[:, 0:2, :]
                           ).then_inc(in_turn, 16)

            pool.wait_ge(table_ready, 1)
            pairs = pool.value_load(tab_pairs[0:1, 0:1], min_val=1, max_val=PAIRS)
            hold(pool, rows_stored, ntiles * 16 + 16, held)
            hold(pool, h2_stored, ntiles * 16 + 16, held)

            def column(g):
                return pool.value_load(tab_col[0:1, bass.ds(g, 1)], min_val=0, max_val=NCH * E - 1)

            def gather(g, u):
                c = column(g)
                steps.mark(nc.gpsimd.tensor_copy(gidx[u][:, :], lists[:, bass.ds(c, 1), 0]))
                steps.wait()
                nc.gpsimd.indirect_dma_start(xg[u].rearrange("p a c -> p (a c)"), None, xn_dram,
                                             bass.IndirectOffsetOnAxis(ap=gidx[u][:, 0:1], axis=0),
                                             bounds_check=ROWS + P - 1, oob_is_err=False).then_inc(xg_in[u], 16)

            def scatter(g, u):
                c = column(g)
                steps.mark(nc.gpsimd.tensor_copy(sidx[u][:, :], lists[:, bass.ds(c, 1), 0]))
                steps.wait()
                nc.gpsimd.indirect_dma_start(y_dram, bass.IndirectOffsetOnAxis(ap=sidx[u][:, 0:1], axis=0), y[u],
                                             None, bounds_check=ROWS + P - 1, oob_is_err=True,
                                             compute_op=ALU.add).then_inc(in_turn, 16)

            pool.wait_ge(in_turn, 16)
            gather(0, 0)
            gather(1, 1)
            pool.wait_ge(other_lists_in, 16)
            pool.wait_ge(xgT_psum, 1)
            pool.wait_ge(xg_in[0], 16)
            gather(2, 0)
            steps.restart()
            with pool.Fori(0, pairs) as m:
                for u in range(2):
                    g = m * 2 + u
                    pool.wait_ge(xgT_psum, g + 2)
                    hold(pool, xg_in[1 - u], m * 16 + 16 + 16 * u, held)
                    gather(g + 3, 1 - u)
                    pool.wait_ge(y_ready, g + 3)
                    pool.wait_ge(in_turn, g * 16 + 16)
                    pool.sem_inc(y_free, 1)
                    scatter(g, u)
                steps.restart()
            hold(pool, in_turn, pairs * 32 + 16, held)
            for u in range(2):
                hold(pool, xg_in[u], pairs * 16 + 32 - 16 * u, held)

        @block.scalar
        def _(act):
            steps = Chain(act, act_steps)
            act.sem_inc(lexp_ready, 1)
            outs = [delta[:, :]] + [wqT[:, c, :] for c in range(C)]
            outs += [wkvT[:, 2 * i:2 * i + 2, :].rearrange("p a b -> p (a b)") for i in range(2)]
            outs += [woT[:, c, :] for c in range(C)] + [gwT[:, :, :].rearrange("p c e -> p (c e)")]
            assert len(outs) == PREP
            for i, o in enumerate(outs):
                act.wait_ge(prep_psum, i + 1)
                nc.scalar.copy(o, bank[i % 4][0:o.shape[0], 0:o.shape[1]]).then_inc(prep_out, 1)

            act.wait_ge(ntiles_ready, 1)
            ntiles = act.value_load(ntiles_i[0:1, 0:1], min_val=1, max_val=B)

            def embed_delta(t):
                act.wait_ge(trainedT_psum, t + 1)
                nc.scalar.copy(trainedT[:, :], bank[3][0:NTRAIN, 128:256]).then_inc(trainedT_ready, 1)

            def embed_transposed(t):
                act.wait_ge(xn1T_psum, t + 1)
                nc.scalar.copy(xn1T.rearrange("p c t -> p (c t)"), bank[3][:, :]).then_inc(xn1T_ready, 1)

            def queries(t):
                act.wait_ge(q_psum, t + 1)
                for f in range(HALVES):
                    last = nc.scalar.mul(q_pad[:, f, :, :, 0:DH], bank[2][:, f * 256:f * 256 + 256]
                                         .rearrange("p (i r d) -> p r i d", r=R, d=DH), DH ** -0.5)
                last.then_inc(q_ready, 1)

            def keys_values(t):
                act.wait_ge(kv_psum, t + 1)
                nc.scalar.mul(v_aug[:, :, 0:DH], bank[0][:, KVD:2 * KVD].rearrange("p (g d) -> p g d", d=DH),
                              rec[:, 2:3])
                nc.scalar.mul(v_aug[:, :, DH], ones[:, 0:G], rec[:, 2:3])
                for f in range(HALVES):
                    last = nc.scalar.copy(k_pad[:, f, :, 0:DH], bank[0][:, f * 64:f * 64 + 64]
                                          .rearrange("p (i d) -> p i d", d=DH))
                last.then_inc(kv_ready, 1)

            def transposed_queries(t):
                act.wait_ge(qkT_psum, t + 1)
                for f in range(HALVES):
                    nc.scalar.copy(qT[:, f, :, :].rearrange("p r t -> p (r t)"), bank[f][:, :]).then_inc(qT_ready, 1)
                nc.scalar.copy(h[:, :], h_next).then_inc(h_ready, 1)

            def transposed_probs(n, g):
                act.wait_ge(probsT_psum, n * G + g + 1)
                nc.scalar.copy(probsT[:, g % 2, :, :].rearrange("p r t -> p (r t)"), bank[4 + g % 2][:, :]
                               ).then_inc(probsT_act, 1)

            embed_delta(0)
            embed_transposed(0)
            queries(0)
            keys_values(0)
            transposed_queries(0)
            with act.Fori(0, ntiles) as n:
                for g in range(G):
                    act.wait_ge(max_ready, n * G + g + 1)
                    if g >= 2:
                        act.wait_ge(probsT_psum, n * G + g - 1)
                    for i in range(4):
                        last = nc.scalar.activation(probs[:, g % 2, i, :],
                                                    bank[SCORE_BANKS[g % 3]][:, i * P:(i + 1) * P], ACT.Exp,
                                                    bias=negmax[:, g, i:i + 1])
                    last.then_inc(probs_ready, 1)
                    if g == 0:
                        embed_delta(n + 1)
                    if g - 1 in BY_ACT:
                        transposed_probs(n, g - 1)
                transposed_probs(n, G - 1)
                embed_transposed(n + 1)
                act.wait_ge(attnT_psum, n + 1)
                nc.scalar.copy(xnT[:, :, :].rearrange("p c t -> p (c t)"), bank[4][:, :]).then_inc(attnT_ready, 1)
                queries(n + 1)
                keys_values(n + 1)
                act.wait_ge(xn2T_psum, n + 1)
                nc.scalar.copy(xnT[:, :, :].rearrange("p c t -> p (c t)"), bank[4][:, :]).then_inc(xn2T_ready, 1)
                transposed_queries(n + 1)
                act.wait_ge(lmax_ready, n + 1)
                nc.scalar.activation(lexp[:, :], bank[5][:, 0:E], ACT.Exp, bias=lmax[:, 0:1],
                                     accum_out=lsum[:, 0:1]).then_inc(lexp_ready, 1)

            nc.scalar.activation(silu[:, 0:1], ones[:, 0:1], ACT.Silu).then_inc(silu_ready, 1)
            act.wait_ge(table_ready, 1)
            pairs = act.value_load(tab_pairs[0:1, 0:1], min_val=1, max_val=PAIRS)

            def transposed_rows(g, u):
                act.wait_ge(xgT_psum, g + 1)
                nc.scalar.copy(xgT[u].rearrange("p c t -> p (c t)"), bank[u][:, :]).then_inc(xgT_ready, 1)

            def silu_gate(g, u, after=True):
                if after:
                    act.wait_ge(hid_ready, g)
                act.wait_ge(gu_psum, g + 1)
                nc.scalar.activation(silu[:, :], bank[2 + u][:, 0:I], ACT.Silu).then_inc(silu_ready, 1)

            transposed_rows(0, 0)
            silu_gate(0, 0, after=False)
            transposed_rows(1, 1)
            with act.Fori(0, pairs) as m:
                for u in range(2):
                    g = m * 2 + u
                    silu_gate(g + 1, 1 - u)
                    transposed_rows(g + 2, u)
            for b in range(0, B, 2):
                if b >= 4:
                    act.wait_ge(final_out[b % 4], 16 * (b // 4))
                act.wait_ge(final_psum, b + 1)
                nc.scalar.copy(final[b % 4], bank[4 + b % 4][:, :]).then_inc(final_even, 1)

        @block.vector
        def _(dve):
            steps = Chain(dve, dve_steps)
            dve.sem_inc(y_ready, 2)
            step, wait = steps.mark, steps.wait
            ts, tt, stt, red = (nc.vector.tensor_scalar, nc.vector.tensor_tensor, nc.vector.scalar_tensor_tensor,
                                nc.vector.tensor_reduce)
            dve.wait_ge(ids_in, 48)
            for raw, ids in ((ids_row_i, scratch), (ids_col_i, ids_col), (train_i, train)):
                step(ts(ids[:, :], raw[:, :], 0.0, float(VOCAB), ALU.is_lt, ALU.mult))
                wait()
                step(tt(ids[:, :], ids[:, :], raw[:, :], ALU.add))
                wait()
                if ids is not train:
                    step(ts(ids[:, :], ids[:, :], float(VOCAB - 1), 0.0, ALU.min, ALU.max))
                    wait()
            dve.wait_ge(consts, 1)
            same_v = same[:, :].rearrange("p (b j) -> p b j", b=B)
            before_v = same_before[:, :].rearrange("p (b j) -> p b j", b=B)
            ids_v = scratch[:, :].rearrange("p (b j) -> p b j", b=B)
            tt(same_v, ids_v, ids_col[:, :].unsqueeze(2).broadcast_to([P, B, S]), ALU.is_equal).then_inc(same_ready, 1)
            dve.wait_ge(same_ready, 1)
            tt(before_v, same_v, earlier_b[:, :].unsqueeze(1).broadcast_to([P, B, S]), ALU.mult
               ).then_inc(before_ready, 1)
            dve.wait_ge(seen_psum, 1)
            ts(first[:, :], bank[5][:, 0:B], 0.0, None, ALU.is_equal).then_inc(first_ready, 1)
            step(nc.vector.tensor_copy(attrs[:, :, 2], bank[4][:, 0:B]))
            step(nc.vector.tensor_copy(ids_col_i[:, :], ids_col[:, :]))
            wait()
            step(ts(low[:, :], ids_col_i[:, :], 255, None, ALU.bitwise_and))
            step(ts(high[:, :], ids_col_i[:, :], 8, None, ALU.logical_shift_right))
            wait()
            step(nc.vector.tensor_copy(attrs[:, :, 0], high[:, :]))
            step(nc.vector.tensor_copy(attrs[:, :, 1], low[:, :]))
            step(ts(attrs[:, :, 3], col[:, 0:B], 1.0, None, ALU.add))
            dve.wait_ge(ranks_psum, 1)
            step(nc.vector.tensor_copy(rank_in_seq[:, :], bank[7][:, 0:B]))
            step(nc.vector.tensor_copy(distinct[:, :], bank[7][:, 64:64 + B]))
            step(nc.vector.memset(fill[:, 0:1], 0.0))
            wait()
            for b in range(B):
                step(ts(keep[:, b:b + 1], distinct[:, b:b + 1], fill[:, b:b + 1], float(P), ALU.add, ALU.is_le))
                wait()
                step(stt(out=fill[:, b + 1:b + 2], in0=fill[:, b:b + 1], scalar=keep[:, b:b + 1],
                         in1=distinct[:, b:b + 1], op0=ALU.mult, op1=ALU.add))
                wait()
            step(ts(keep[:, :], keep[:, :], -1.0, 1.0, ALU.mult, ALU.add))
            wait()
            step(nc.vector.tensor_tensor_scan(skips[:, :], keep[:, :], zeros[:, 0:B], 0.0, ALU.add, ALU.add))
            wait()
            ins = ts(ntiles_i[0:1, 0:1], skips[0:1, B - 1:B], 1.0, None, ALU.add)
            ins.then_inc(ntiles_ready, 1)
            step(stt(out=offset[:, :], in0=skips[:, :], scalar=float(P), in1=fill[:, 1:B + 1], op0=ALU.mult,
                     op1=ALU.add))
            wait()
            step(tt(offset[:, :], offset[:, :], distinct[:, :], ALU.subtract))
            wait()
            step(tt(slot_of[:, :], offset[:, :], rank_in_seq[:, :], ALU.add))
            wait()
            step(stt(out=first_slot[:, :], in0=slot_of[:, :], scalar=1.0, in1=first[:, :], op0=ALU.add, op1=ALU.mult))
            wait()
            step(tt(chosen[:, :], slot_of[:, :], first[:, :], ALU.mult))
            step(ts(first_slot[:, :], first_slot[:, :], -1.0, None, ALU.add))
            dve.wait_ge(ntiles_ready, 1)
            ntiles = dve.value_load(ntiles_i[0:1, 0:1], min_val=1, max_val=B)
            dve.wait_ge(prep_out, PREP)
            steps.restart()

            def pick_tokens(t):
                tt(pick[:, :, :], first_slot[:, :].unsqueeze(2).broadcast_to([P, B, P]),
                   col[:, 0:P].unsqueeze(1).broadcast_to([P, B, P]), ALU.is_equal).then_inc(pick_ready, 1)
                dve.wait_ge(pick_ready, t + 1)
                step(ts(first_slot[:, :], first_slot[:, :], -float(P), None, ALU.add))

            def embed_ids(t):
                dve.wait_ge(rec_psum, t + 1)
                step(nc.vector.tensor_copy(rec[:, :], bank[3][:, 0:4]))
                wait()
                step(stt(out=id_f[:, :], in0=rec[:, 0:1], scalar=256.0, in1=rec[:, 1:2], op0=ALU.mult, op1=ALU.add))
                wait()
                nc.vector.tensor_copy(id_i[:, :], id_f[:, :]).then_inc(id_ready, 1)
                ts(trained[:, 0:NTRAIN], train[:, :], id_f[:, 0:1], None, ALU.is_equal).then_inc(trained_ready, 1)

            def embed_sequences():
                step(ts(seq_is[:, :], col[:, 1:B + 1], rec[:, 3:4], None, ALU.is_equal))
                step(nc.vector.tensor_copy(valid_now[:, :], valid_next[:, :]))
                wait()
                step(ts(k_pad[:, :, :, DH:32].rearrange("p f i d -> p (f i) d"),
                        seq_is[:, :].unsqueeze(1).broadcast_to([P, G, B]), -1.0, None, ALU.add))
                step(ts(q_pad[:, :, :, :, DH:32].rearrange("p f r i d -> p (f r i) d"),
                        seq_is[:, :].unsqueeze(1).broadcast_to([P, H, B]), MASK, None, ALU.mult))
                step(ts(valid_next[:, :], rec[:, 2:3], 0.0, None, ALU.is_gt))

            def moments(src):
                step(nc.vector.bn_stats(stats[:, 0, :], src))
                wait()
                mean_variance(1)

            def mean_variance(parts):
                step(nc.vector.bn_aggr(mv[:, :], stats[:, 0:parts, :].rearrange("p a s -> p (a s)")))
                wait()
                ts(var_eps[:, :], mv[:, 1:2], EPS, None, ALU.add).then_inc(var_ready, 1)

            def normalise(dst, src, k, ready):
                dve.wait_ge(rstd_ready, k)
                ts(dst, src, mv[:, 0:1], rstd[:, 0:1], ALU.subtract, ALU.mult).then_inc(ready, 1)

            def embed_rows(t):
                dve.wait_ge(row_gathered, t * 16 + 16)
                dve.wait_ge(delta_psum, t + 1)
                step(tt(h_next, w_row[:, :], bank[3][:, :], ALU.add))
                wait()
                moments(h_next)

            def transposed_keys(t):
                dve.wait_ge(qkT_psum, t + 1)
                for f in range(HALVES):
                    for i in range(4):
                        last = nc.vector.tensor_copy(kT[i * 32:i * 32 + 32, f, i, :],
                                                     bank[2][i * 32:i * 32 + 32, f * P:(f + 1) * P])
                    last.then_inc(kT_ready, 1)

            def route_top(k):
                dve.wait_ge(lexp_ready, k + 1)
                step(nc.vector.reciprocal(lrec[:, :], lsum[:, :]))
                wait()
                step(ts(score[:, :], lexp[:, :], lrec[:, 0:1], None, ALU.mult))
                wait()
                step(nc.vector.max(top[:, :], score[:, :]))
                wait()
                step(nc.vector.max_index(top_i[:, :], top[:, :], score[:, :]))
                step(red(topsum[:, :], top[:, :], X, ALU.add))
                wait()
                step(nc.vector.reciprocal(toprec[:, :], topsum[:, :]))
                step(nc.vector.tensor_copy(top_f[:, :], top_i[:, :]))
                wait()

            def route_mask(k):
                step(tt(is_e[:, :, :], col[:, 0:E].unsqueeze(1).broadcast_to([P, TOPK, E]),
                        top_f[:, :].unsqueeze(2).broadcast_to([P, TOPK, E]), ALU.is_equal))
                wait()
                step(red(mask[:, :], is_e[:, :, :].rearrange("p k e -> p e k"), X, ALU.add))
                wait()
                ts(mask_b[:, :], mask[:, :], valid[:, 0:1], None, ALU.mult).then_inc(mask_ready, 1)

            def route_ranks(k):
                dve.wait_ge(rank_psum, k + 1)
                step(tt(rank[:, :], taken[:, :], bank[7][:, 0:E], ALU.add))
                wait()
                step(tt(taken[:, :], taken[:, :], bank[7][:, E:2 * E], ALU.add))

            def route_lists(k):
                step(tt(picked[:, :, :], is_e[:, :, :], rank[:, :].unsqueeze(1).broadcast_to([P, TOPK, E]), ALU.mult))
                step(ts(far[:, :], valid[:, :], -FAR, FAR, ALU.mult, ALU.add))
                wait()
                step(red(rank_k[:, :], picked[:, :, :], X, ALU.add))
                wait()
                step(stt(out=dest_f[:, :], in0=rank_k[:, :], scalar=float(E), in1=top_f[:, :], op0=ALU.mult,
                         op1=ALU.add))
                wait()
                dve.wait_ge(lists_free, k + 1)
                step(ts(dest[:, :], dest_f[:, :], far[:, 0:1], None, ALU.add))
                step(nc.vector.tensor_copy(list_rec[:, :, 0], my_slot[:, :].broadcast_to([P, TOPK])))
                step(ts(list_rec[:, :, 1].bitcast(F32), top[:, :], toprec[:, 0:1], None, ALU.mult))
                step(nc.vector.tensor_copy(valid[:, :], valid_now[:, :]))
                wait()
                ts(my_slot[:, :], my_slot[:, :], float(P), None, ALU.add).then_inc(list_ready, 1)

            pick_tokens(0)
            embed_ids(0)
            embed_sequences()
            pick_tokens(1)
            step(nc.vector.memset(kT, 0.0))
            step(ts(chosen_low[:, :], chosen[:, :], P - 1, None, ALU.bitwise_and))
            step(nc.vector.tensor_copy(tab_tile[:, :], skips[0:1, :]))
            wait()
            step(stt(out=place[:, :], in0=chosen_low[:, :], scalar=1.0, in1=first[:, :], op0=ALU.add, op1=ALU.mult))
            wait()
            step(ts(place[:, :], place[:, :], -1.0, None, ALU.add))
            embed_rows(0)
            normalise(xn1, h_next, 1, xn1_ready)
            transposed_keys(0)
            steps.restart()
            with dve.Fori(0, ntiles) as n:
                def row_max(g):
                    dve.wait_ge(scores_psum, n * G + g + 1)
                    step(red(negmax[:, g, :], bank[SCORE_BANKS[g % 3]][:, :].rearrange("p (i k) -> p i k", i=4), X,
                             ALU.max))
                    wait()
                    ts(negmax[:, g, :], negmax[:, g, :], -1.0, None, ALU.mult).then_inc(max_ready, 1)

                row_max(0)
                dve.wait_ge(kv_ready, n + 1)
                embed_ids(n + 1)
                for g in (1, 2):
                    row_max(g)
                embed_sequences()
                for g in range(G):
                    if g in BY_DVE:
                        dve.wait_ge(probsT_psum, n * G + g + 1)
                        nc.vector.tensor_copy(probsT[:, g % 2, :, :].rearrange("p r t -> p (r t)"),
                                              bank[4 + g % 2][:, :]).then_inc(probsT_dve, 1)
                    if g + 3 < G:
                        row_max(g + 3)
                    if g == 0:
                        route_top(n)
                    if g == 1:
                        route_mask(n)
                    if g == 3:
                        route_ranks(n)
                    if g == 4:
                        dve.wait_ge(h_ready, n + 1)
                        embed_rows(n + 1)
                    if g == 5:
                        normalise(xn1, h_next, n * 2 + 2, xn1_ready)
                        route_lists(n)
                dve.wait_ge(attn_psum, n + 1)
                for f in range(HALVES):
                    o = bank[6 + f][:, 0:16 * 17].rearrange("p (h d) -> p h d", d=17)
                    step(nc.vector.reciprocal(rden[:, f * 16:f * 16 + 16], o[:, :, DH]))
                wait()
                for f in range(HALVES):
                    o = bank[6 + f][:, 0:16 * 17].rearrange("p (h d) -> p h d", d=17)
                    last = tt(attn[:, f * 16:f * 16 + 16, :], o[:, :, 0:DH],
                              rden[:, f * 16:f * 16 + 16].unsqueeze(2).broadcast_to([P, 16, DH]), ALU.mult)
                last.then_inc(attn_ready, 1)
                pick_tokens(n + 2)
                dve.wait_ge(h2_stored, n * 16 + 16)
                for half in range(2):
                    cols = slice(half * D // 2, (half + 1) * D // 2)
                    dve.wait_ge(proj_psum, n * 2 + half + 1)
                    tt(h2[:, cols], h[:, cols], bank[5 - half][:, 0:D // 2], ALU.add).then_inc(h2_ready, 1)
                    dve.wait_ge(h2_ready, n * 2 + half + 1)
                    step(nc.vector.bn_stats(stats[:, half, :], h2[:, cols]))
                wait()
                mean_variance(2)
                dve.wait_ge(rows_stored, n * 16 + 16)
                normalise(xn[:, :], h2[:, :], n * 2 + 3, xn2_ready)
                transposed_keys(n + 1)
                dve.wait_ge(logits_psum, n + 1)
                step(red(lmax[:, :], bank[5][:, 0:E], X, ALU.max))
                wait()
                ts(lmax[:, :], lmax[:, :], -1.0, None, ALU.mult).then_inc(lmax_ready, 1)
                steps.restart()

            route_top(ntiles)
            route_mask(ntiles)
            route_ranks(ntiles)
            route_lists(ntiles)
            wait()
            dve.wait_ge(counts_psum, 1)
            step(nc.vector.tensor_copy(count_e[:, :], bank[0][0:E, 0:1]))
            wait()
            step(ts(more[:, :], tile_starts[0:E, :], count_e[:, 0:1], None, ALU.is_lt))
            wait()
            step(red(tiles_e[:, :], more[:, :], X, ALU.add))
            wait()
            ts(tiles_eb[:, :], tiles_e[:, :], 1.0, None, ALU.max).then_inc(tiles_ready, 1)
            dve.wait_ge(upto_psum, 1)
            step(nc.vector.tensor_copy(upto_e[:, :], bank[1][0:E, 0:1]))
            wait()
            ts(past[:, :], col[0:E, 0:TILES], upto_e[:, 0:1], None, ALU.is_ge).then_inc(past_ready, 1)
            dve.wait_ge(table_psum, 1)
            step(nc.vector.tensor_copy(t_exp[:, :], bank[2][0:1, 0:TILES]))
            step(nc.vector.tensor_copy(t_used[:, :], bank[3][0:1, 0:TILES]))
            step(ts(total_i[:, :], bank[4][0:1, 0:1], 1.0, None, ALU.add))
            step(nc.vector.tensor_copy(tab_upto[:, :], bank[5][0:1, 0:E]))
            wait()
            step(ts(t_end[:, :], t_exp[:, :], float(E), None, ALU.is_ge))
            step(tt(t_col[:, :], col[0:1, 0:TILES], t_used[:, :], ALU.subtract))
            step(ts(tab_pairs[:, :], total_i[:, :], 1, None, ALU.logical_shift_right))
            wait()
            step(stt(out=t_col[:, :], in0=t_col[:, :], scalar=float(E), in1=t_exp[:, :], op0=ALU.mult, op1=ALU.add))
            step(ts(t_exp[:, :], t_exp[:, :], float(E - 1), None, ALU.min))
            wait()
            step(ts(t_used[:, :], t_end[:, :], -1.0, 1.0, ALU.mult, ALU.add))
            step(nc.vector.tensor_copy(t_slot[:, :], t_exp[:, :]))
            step(ts(tab_exp[:, :], t_exp[:, :], 1.0, None, ALU.add))
            wait()
            step(tt(t_col[:, :], t_col[:, :], t_used[:, :], ALU.mult))
            step(ts(tab_slot[:, :], t_slot[:, :], SLOTS - 1, None, ALU.bitwise_and))
            wait()
            stt(out=tab_col[:, :], in0=t_end[:, :], scalar=float((NCH - 1) * E), in1=t_col[:, :], op0=ALU.mult,
                op1=ALU.add).then_inc(table_ready, 1)
            tt(pick[:, :, :], place[:, :].unsqueeze(2).broadcast_to([P, B, P]),
               col[:, 0:P].unsqueeze(1).broadcast_to([P, B, P]), ALU.is_equal).then_inc(places_ready, 1)
            hold(dve, h_ready, ntiles + 1, held)
            for i in range(4):
                dve.wait_ge(onehot_psum, i + 1)
                nc.vector.tensor_copy(onehot[:, i * 512:(i + 1) * 512], bank[6 + i % 2][:, :]).then_inc(onehot_ready, 1)
            dve.wait_ge(table_ready, 1)
            dve.wait_ge(in_turn, 16)
            pairs = dve.value_load(tab_pairs[0:1, 0:1], min_val=1, max_val=PAIRS)

            def gate(g, u):
                c = dve.value_load(tab_col[0:1, bass.ds(g, 1)], min_val=0, max_val=NCH * E - 1)
                dve.wait_ge(silu_ready, g + 2)
                stt(out=hid[u][:, :, :].rearrange("p a c -> p (a c)"), in0=bank[2 + u][:, I:2 * I],
                    scalar=lists[:, bass.ds(c, 1), 1].bitcast(F32), in1=silu[:, :], op0=ALU.mult,
                    op1=ALU.mult).then_inc(hid_ready, 1)

            gate(0, 0)
            dve.wait_ge(other_lists_in, 16)
            steps.restart()
            with dve.Fori(0, pairs) as m:
                for u in range(2):
                    g = m * 2 + u
                    dve.wait_ge(hidT_psum, g + 1)
                    nc.vector.tensor_copy(hidT[u][:, :, :].rearrange("p c t -> p (c t)"),
                                          bank[4 + u][0:IP, 0:IC * P]).then_inc(hidT_ready, 1)
                    gate(g + 1, 1 - u)
                    dve.wait_ge(y_free, g + 1)
                    dve.wait_ge(y_psum, g + 1)
                    nc.vector.tensor_copy(y[u], bank[6 + u][:, :]).then_inc(y_ready, 1)
                steps.restart()
            for b in range(1, B, 2):
                if b >= 4:
                    dve.wait_ge(final_out[b % 4], 16 * (b // 4))
                dve.wait_ge(final_psum, b + 1)
                nc.vector.tensor_copy(final[b % 4], bank[4 + b % 4][:, :]).then_inc(final_odd, 1)

        @block.tensor
        def _(pe):
            mm, tr = nc.tensor.matmul, nc.tensor.transpose
            pe.wait_ge(consts, 1)
            def keep_warm(dst, times):
                for _ in range(times):
                    mm(dst[:, :], wqT[:, 0, 0:P], wqT[:, 0, :], start=True, stop=True)

            for src, ready, dst in ((same, same_ready, bank[4]), (same_before, before_ready, bank[5])):
                pe.wait_ge(ready, 1)
                for b in range(B):
                    last = mm(dst[:, b:b + 1], src[:, b * S:(b + 1) * S], ones_b[:, 0:1], start=True, stop=True)
            last.then_inc(seen_psum, 1)
            pe.wait_ge(first_ready, 1)
            mm(bank[7][:, 0:B], earlier[:, :], first[:, :], start=True, stop=True)
            mm(bank[7][:, 64:64 + B], ones[:, :], first[:, :], start=True, stop=True).then_inc(ranks_psum, 1)
            groups = [[(delta_nat[:, c, :], NTRAIN, c * P) for c in range(C)]]
            groups += [[(wq_nat[:, r, c * P:(c + 1) * P], P, r * P) for r in range(C)] for c in range(C)]
            groups += [[(wkv_nat[:, s, c * P:(c + 1) * P], P, (c % 2) * 2 * P + s * P) for c in (2 * i, 2 * i + 1)
                        for s in range(2)] for i in range(2)]
            groups += [[(wo_nat[:, r, c * P:(c + 1) * P], P, r * P) for r in range(C)] for c in range(C)]
            groups += [[(gw_nat[:, c * P:(c + 1) * P], P, c * E) for c in range(C)]]
            pe.wait_ge(weights_in, 96)
            for i, pieces in enumerate(groups):
                if i >= 4:
                    pe.wait_ge(prep_out, i - 3)
                for src, rows, at in pieces:
                    k = src.shape[0]
                    last = tr(bank[i % 4][0:rows, at:at + k], src, ident[0:k, 0:k])
                last.then_inc(prep_psum, 1)
            pe.wait_ge(ntiles_ready, 1)
            ntiles = pe.value_load(ntiles_i[0:1, 0:1], min_val=1, max_val=B)
            pe.wait_ge(prep_out, PREP)

            def embed_records(t):
                pe.wait_ge(pick_ready, t + 1)
                for b in range(B):
                    last = mm(bank[3][:, 0:4], pick[:, b, :], attrs[:, b, :], start=(b == 0), stop=(b == B - 1))
                last.then_inc(rec_psum, 1)

            def embed_trained(t):
                pe.wait_ge(trained_ready, t + 1)
                tr(bank[3][:, 128:256], trained[:, :], ident[:, :]).then_inc(trainedT_psum, 1)

            def embed_delta(t):
                pe.wait_ge(trainedT_ready, t + 1)
                mm(bank[3][:, :], trainedT[:, :], delta[:, :], start=True, stop=True).then_inc(delta_psum, 1)

            def transpose_rows(src, dst):
                for c in range(C):
                    last = tr(dst[:, c * P:(c + 1) * P], src[:, c * P:(c + 1) * P], ident[:, :])
                return last

            def embed_transposed(t):
                pe.wait_ge(xn1_ready, t + 1)
                transpose_rows(xn1, bank[3]).then_inc(xn1T_psum, 1)

            def queries(t, chunks):
                if chunks[0] == 0:
                    pe.wait_ge(xn1T_ready, t + 1)
                for c in chunks:
                    last = mm(bank[2][:, :], xn1T[:, c, :], wqT[:, c, :], start=(c == 0), stop=(c == C - 1))
                if c == C - 1:
                    last.then_inc(q_psum, 1)

            def keys_values(t):
                for c in range(C):
                    last = mm(bank[0][:, 0:2 * KVD], xn1T[:, c, :], wkvT[:, c, :], start=(c == 0), stop=(c == C - 1))
                last.then_inc(kv_psum, 1)

            def transpose_queries(t):
                pe.wait_ge(q_ready, t + 1)
                pe.wait_ge(kv_ready, t + 1)
                for f in range(HALVES):
                    for r in range(R):
                        tr(bank[f][:, r * P:(r + 1) * P], q_pad[:, f, r, :, :].rearrange("p i d -> p (i d)"),
                           ident[:, :])
                    last = tr(bank[2][:, f * P:(f + 1) * P], k_pad[:, f, :, :].rearrange("p i d -> p (i d)"),
                              ident[:, :])
                last.then_inc(qkT_psum, 1)

            def list_ranks(k):
                pe.wait_ge(mask_ready, k + 1)
                mm(bank[7][:, 0:E], earlier_b[:, :], mask_b[:, :], start=True, stop=True)
                mm(bank[7][:, E:2 * E], ones_b[:, :], mask_b[:, :], start=True, stop=True).then_inc(rank_psum, 1)

            embed_records(0)
            embed_trained(0)
            embed_delta(0)
            keep_warm(bank[6], 3)
            embed_transposed(0)
            keep_warm(bank[6], 1)
            queries(0, range(C))
            keys_values(0)
            keep_warm(bank[6], 2)
            transpose_queries(0)
            embed_records(1)
            keep_warm(bank[6], 1)
            with pe.Fori(0, ntiles) as n:
                def scores(g):
                    f, r = g // R, g % R
                    mm(bank[SCORE_BANKS[g % 3]][:, :], qT[:, f, r, :], kT[:, f, :, :].rearrange("p i t -> p (i t)"),
                       start=True, stop=True).then_inc(scores_psum, 1)

                def transpose_probs(g):
                    pe.wait_ge(probs_ready, n * G + g + 1)
                    for i in range(4):
                        last = tr(bank[4 + g % 2][:, i * P:(i + 1) * P], probs[:, g % 2, i, :], ident[:, :])
                    last.then_inc(probsT_psum, 1)

                for g in range(3):
                    if g == 0:
                        pe.wait_ge(qT_ready, n * 2 + 1)
                        pe.wait_ge(kT_ready, n * 2 + 1)
                    if g == 1:
                        pe.wait_ge(kT_ready, n * 2 + 2)
                    if g == 2:
                        pe.wait_ge(qT_ready, n * 2 + 2)
                    scores(g)
                embed_trained(n + 1)
                transpose_probs(0)
                for g in range(G):
                    if g + 3 < G:
                        scores(g + 3)
                    if g == 0:
                        embed_delta(n + 1)
                    if g + 1 < G:
                        transpose_probs(g + 1)
                    if g == 2:
                        list_ranks(n)
                    if g in BY_DVE:
                        pe.wait_ge(probsT_dve, n * len(BY_DVE) + BY_DVE.index(g) + 1)
                    else:
                        pe.wait_ge(probsT_act, n * len(BY_ACT) + BY_ACT.index(g) + 1)
                    f, r = g // R, g % R
                    for i in range(4):
                        hd = i * R + r
                        last = mm(bank[6 + f][:, hd * 17:hd * 17 + 17], probsT[:, g % 2, i, :], v_aug[:, f * 4 + i, :],
                                  start=True, stop=True)
                    if g == 6:
                        embed_transposed(n + 1)
                last.then_inc(attn_psum, 1)
                queries(n + 1, (0, 1))
                pe.wait_ge(attn_ready, n + 1)
                transpose_rows(attn[:, :, :].rearrange("p h d -> p (h d)"), bank[4]).then_inc(attnT_psum, 1)
                queries(n + 1, (2,))
                pe.wait_ge(attnT_ready, n + 1)
                for half in range(2):
                    for c in range(C):
                        last = mm(bank[5 - half][:, 0:D // 2], xnT[:, c, :],
                                  woT[:, c, half * D // 2:(half + 1) * D // 2],
                                  start=(c == 0), stop=(c == C - 1))
                    last.then_inc(proj_psum, 1)
                queries(n + 1, (3,))
                keys_values(n + 1)
                pe.wait_ge(xn2_ready, n + 1)
                transpose_rows(xn, bank[4]).then_inc(xn2T_psum, 1)
                transpose_queries(n + 1)
                embed_records(n + 2)
                pe.wait_ge(xn2T_ready, n + 1)
                for c in range(C):
                    last = mm(bank[5][:, 0:E], xnT[:, c, :], gwT[:, c, :], start=(c == 0), stop=(c == C - 1))
                last.then_inc(logits_psum, 1)

            list_ranks(ntiles)
            hold(pe, list_ready, ntiles + 1, held)
            hold(pe, qT_ready, ntiles * 2 + 2, held)
            tr(bank[0][0:E, 0:P], taken[:, :], ident[:, :]).then_inc(counts_psum, 1)
            pe.wait_ge(tiles_ready, 1)
            mm(bank[1][0:E, 0:1], upto[0:E, 0:E], tiles_eb[:, :], start=True, stop=True).then_inc(upto_psum, 1)
            pe.wait_ge(past_ready, 1)
            mm(bank[2][0:1, 0:TILES], ones_b[0:E, 0:1], past[:, :], start=True, stop=True)
            mm(bank[3][0:1, 0:TILES], tiles_eb[:, :], past[:, :], start=True, stop=True)
            mm(bank[4][0:1, 0:1], ones_b[0:E, 0:1], tiles_eb[:, :], start=True, stop=True)
            mm(bank[5][0:1, 0:E], tiles_eb[:, :], upto[0:E, 0:E], start=True, stop=True).then_inc(table_psum, 1)
            pe.wait_ge(places_ready, 1)
            for i in range(4):
                if i >= 2:
                    pe.wait_ge(onehot_ready, i - 1)
                for b in range(4 * i, 4 * i + 4):
                    last = mm(bank[6 + i % 2][:, b % 4 * S:(b % 4 + 1) * S], pick[:, b, :], same[:, b * S:(b + 1) * S],
                              start=True, stop=True)
                last.then_inc(onehot_psum, 1)
            pe.wait_ge(onehot_ready, 4)
            pe.wait_ge(in_turn, 16)
            keep_warm(bank[7], 5)
            pe.wait_ge(table_ready, 1)
            pairs = pe.value_load(tab_pairs[0:1, 0:1], min_val=1, max_val=PAIRS)

            def transpose_gathered(g, u, turn):
                pe.wait_ge(xg_in[u], turn * 16)
                for c in range(C):
                    last = tr(bank[u][:, c * P:(c + 1) * P], xg[u][:, :, c], ident[:, :])
                last.then_inc(xgT_psum, 1)

            def slot_of_tile(g):
                return pe.value_load(tab_slot[0:1, bass.ds(g, 1)], min_val=0, max_val=SLOTS - 1)

            def expert_of_tile(g):
                return pe.value_load(tab_exp[0:1, bass.ds(g, 1)], min_val=1, max_val=E)

            def gate_up(g, u, slot, need):
                pe.wait_ge(expert_in, need)
                pe.wait_ge(xgT_ready, g + 1)
                for c in range(C):
                    last = mm(bank[2 + u][:, 0:2 * I], xgT[u][:, c, :],
                              wgu[:, bass.ds(slot, 1), :, c * I:(c + 1) * I].rearrange("p o w i -> p (o w) i"),
                              start=(c == 0), stop=(c == C - 1))
                last.then_inc(gu_psum, 1)

            transpose_gathered(0, 0, 1)
            gate_up(0, 0, slot_of_tile(0), expert_of_tile(0))
            transpose_gathered(1, 1, 1)
            with pe.Fori(0, pairs) as m:
                for u in range(2):
                    g = m * 2 + u
                    slot = slot_of_tile(g) if u == 0 else slot_next
                    slot_next, expert_next = slot_of_tile(g + 1), expert_of_tile(g + 1)
                    pe.wait_ge(hid_ready, g + 1)
                    for c in range(IC):
                        last = tr(bank[4 + u][0:IP, c * P:(c + 1) * P], hid[u][:, :, c], ident[:, :])
                    last.then_inc(hidT_psum, 1)
                    gate_up(g + 1, 1 - u, slot_next, expert_next)
                    transpose_gathered(g + 2, u, m + 2)
                    pe.wait_ge(hidT_ready, g + 1)
                    pe.wait_ge(y_ready, g + 1)
                    for c in range(IC):
                        last = mm(bank[6 + u][:, :], hidT[u][:, c, :],
                                  wdn[:, bass.ds(slot, 1), c * D:(c + 1) * D].rearrange("p o n -> p (o n)"),
                                  start=(c == 0), stop=(c == IC - 1))
                    last.then_inc(y_psum, 1)

            hold(pe, in_turn, pairs * 32 + 16, held)
            keep_warm(bank[7], 6)
            hold(pe, y_in, ntiles * 16, held)
            for b in range(B):
                tile = pe.value_load(tab_tile[0:1, b:b + 1], min_val=0, max_val=B - 1)
                if b >= 4:
                    pe.wait_ge(final_odd if b % 2 else final_even, b // 2 - 1)
                mm(bank[4 + b % 4][:, :], onehot[:, b * S:(b + 1) * S],
                   y_tiles[:, bass.ds(tile, 1), :].rearrange("p o d -> p (o d)"), start=True, stop=True
                   ).then_inc(final_psum, 1)


_INS = ['x', 'L0_tok_W', 'L0_tok_delta_values', 'L0_tok_token_indices', 'L0_attn_w_q', 'L0_attn_w_k', 'L0_attn_w_v',
        'L0_attn_w_o', 'L0_ffn_gate_weight', 'L0_ffn_w_gate', 'L0_ffn_w_up', 'L0_ffn_w_down']
_OUTS = [((16, 128, 512), 'float32')]
build = dedup_moe_lm_tower


def kernel(**inputs):
    import numpy as _np
    import concourse.bacc as _bacc
    from concourse import mybir as _mybir
    from concourse.bass_utils import run_bass_kernel_spmd as _run

    nc = _bacc.Bacc("TRN2", target_bir_lowering=False, num_devices=1)
    arrays, args = {}, []
    for name in _INS:
        a = _np.ascontiguousarray(inputs[name])
        arrays[f"in_{name}_dram"] = a
        args.append(nc.dram_tensor(f"in_{name}_dram", a.shape, _mybir.dt.from_np(a.dtype), kind="ExternalInput").ap())
    for i, (shape, dtype) in enumerate(_OUTS):
        dt = _mybir.dt.from_np(_np.dtype(dtype))
        args.append(nc.dram_tensor(f"out_{i}_dram", shape, dt, kind="ExternalOutput").ap())
    dedup_moe_lm_tower(nc, *args)
    r = _run(nc, [arrays], core_ids=[0])
    return r.results[0]["out_0_dram"]
```
